# Optimizing a Trainium2 kernel written in Bass

```python
import numpy as np
import jax
import jax.numpy as jnp

def _softmax(x, axis=-1):
    return jax.nn.softmax(x, axis=axis)
def _gelu(x):
    return jax.nn.gelu(x, approximate=True)
def _silu(x):
    return jax.nn.silu(x)
def _sigmoid(x):
    return jax.nn.sigmoid(x)
def _layernorm(x, axis=-1, eps=1e-5):
    m = jnp.mean(x, axis=axis, keepdims=True)
    v = jnp.var(x, axis=axis, keepdims=True)
    return (x - m) / jnp.sqrt(v + eps)
def _scatter_add(tgt, idx, src, axis=0):
    return tgt.at[idx].add(src)
def _segment_sum(src, seg, n):
    return jax.ops.segment_sum(src, seg, n)

kernel_name = 'mk_adj_seq_d4_adj_256_c9ed00'

def setup_inputs(seed: int = 0):
    np.random.seed(seed)
    _w = jnp.asarray
    def _rec_inputs():
        import jax
        import jax.numpy as jnp
        _gk = jax.random.key(seed)
        x = -0.000929 + 1 * jax.random.normal(jax.random.fold_in(_gk, 1), (3327, 256), jnp.float32)
        _a = jax.random.bernoulli(jax.random.fold_in(_gk, 2), 0.00240457, (3327, 3327))
        _a = jnp.logical_or(_a, jnp.eye(3327, dtype=bool))
        adj = _a.astype(jnp.int32)
        return x, adj
    x, adj = _rec_inputs()
    def _L0_gnn_setup():
        import jax, jax.numpy as jnp
        import numpy as np
        DIM = 256
        HEADS = 8
        DIM_FF = 1024
        N = 4096
        HEAD_DIM = DIM // HEADS
        SCALE = HEAD_DIM ** (-0.5)

        def layer_norm(x, gamma, beta, eps=1e-05):
            mu = jnp.mean(x, axis=-1, keepdims=True)
            var = jnp.var(x, axis=-1, keepdims=True)
            return (x - mu) * jax.lax.rsqrt(var + eps) * gamma + beta
        key = jax.random.key(seed)
        ks = jax.random.split(key, 8)
        x = jax.random.normal(ks[0], (N, DIM), dtype=jnp.float32)
        adj = jax.random.randint(ks[1], (N, N), 0, 2, dtype=jnp.int32)
        adj = adj.at[jnp.arange(N), jnp.arange(N)].set(1)
        s = 1.0 / np.sqrt(DIM)
        w_qkv = jax.random.normal(ks[2], (DIM, 3 * DIM), dtype=jnp.float32) * s
        w_proj = jax.random.normal(ks[3], (DIM, DIM), dtype=jnp.float32) * s
        b_proj = jnp.zeros((DIM,), jnp.float32)
        w1 = jax.random.normal(ks[4], (DIM, DIM_FF), dtype=jnp.float32) * s
        b1 = jnp.zeros((DIM_FF,), jnp.float32)
        w2 = jax.random.normal(ks[5], (DIM_FF, DIM), dtype=jnp.float32) / np.sqrt(DIM_FF)
        b2 = jnp.zeros((DIM,), jnp.float32)
        g1 = jnp.ones((DIM,), jnp.float32)
        be1 = jnp.zeros((DIM,), jnp.float32)
        g2 = jnp.ones((DIM,), jnp.float32)
        be2 = jnp.zeros((DIM,), jnp.float32)
        return {'x': x, 'adj': adj, 'w_qkv': w_qkv, 'w_proj': w_proj, 'b_proj': b_proj, 'w1': w1, 'b1': b1, 'w2': w2, 'b2': b2, 'g1': g1, 'be1': be1, 'g2': g2, 'be2': be2}
    _L0_gnn_all = _L0_gnn_setup()
    _L0_gnn_in = {k: v for k, v in _L0_gnn_all.items() if k in ('w_qkv', 'w_proj', 'b_proj', 'w1', 'b1', 'w2', 'b2', 'g1', 'be1', 'g2', 'be2', )}
    del _L0_gnn_all

    def _L1_gnn_setup():
        import jax, jax.numpy as jnp
        import numpy as np
        N = 8192
        F = 256
        H = 64
        NEG = -9000000000000000.0
        EPS = 1e-05
        key = jax.random.key(seed)
        ks = jax.random.split(key, 6)
        x = jax.random.normal(ks[0], (N, F), jnp.float32)
        adj = jax.random.randint(ks[1], (N, N), 0, 2, jnp.int32)
        Wt = jax.random.normal(ks[2], (H, F), jnp.float32) * (1.0 / np.sqrt(F))
        bt = jnp.zeros((H,), jnp.float32)
        Wa = jax.random.normal(ks[3], (1, H), jnp.float32) * (1.0 / np.sqrt(H))
        ba = jnp.zeros((1,), jnp.float32)
        Wp = jax.random.normal(ks[4], (F, H), jnp.float32) * (1.0 / np.sqrt(H))
        bp = jnp.zeros((F,), jnp.float32)
        gamma = jnp.ones((F,), jnp.float32)
        beta = jnp.zeros((F,), jnp.float32)
        return dict(x=x, adj=adj, Wt=Wt, bt=bt, Wa=Wa, ba=ba, Wp=Wp, bp=bp, gamma=gamma, beta=beta)
    _L1_gnn_all = _L1_gnn_setup()
    _L1_gnn_in = {k: v for k, v in _L1_gnn_all.items() if k in ('Wt', 'bt', 'Wa', 'ba', 'Wp', 'bp', 'gamma', 'beta', )}
    del _L1_gnn_all

    def _L2_gnn_setup():
        import jax, jax.numpy as jnp
        import numpy as np
        DIM = 256
        HEADS = 8
        DIM_FF = 1024
        N = 4096
        HEAD_DIM = DIM // HEADS
        SCALE = HEAD_DIM ** (-0.5)

        def layer_norm(x, gamma, beta, eps=1e-05):
            mu = jnp.mean(x, axis=-1, keepdims=True)
            var = jnp.var(x, axis=-1, keepdims=True)
            return (x - mu) * jax.lax.rsqrt(var + eps) * gamma + beta
        key = jax.random.key(seed)
        ks = jax.random.split(key, 8)
        x = jax.random.normal(ks[0], (N, DIM), dtype=jnp.float32)
        adj = jax.random.randint(ks[1], (N, N), 0, 2, dtype=jnp.int32)
        adj = adj.at[jnp.arange(N), jnp.arange(N)].set(1)
        s = 1.0 / np.sqrt(DIM)
        w_qkv = jax.random.normal(ks[2], (DIM, 3 * DIM), dtype=jnp.float32) * s
        w_proj = jax.random.normal(ks[3], (DIM, DIM), dtype=jnp.float32) * s
        b_proj = jnp.zeros((DIM,), jnp.float32)
        w1 = jax.random.normal(ks[4], (DIM, DIM_FF), dtype=jnp.float32) * s
        b1 = jnp.zeros((DIM_FF,), jnp.float32)
        w2 = jax.random.normal(ks[5], (DIM_FF, DIM), dtype=jnp.float32) / np.sqrt(DIM_FF)
        b2 = jnp.zeros((DIM,), jnp.float32)
        g1 = jnp.ones((DIM,), jnp.float32)
        be1 = jnp.zeros((DIM,), jnp.float32)
        g2 = jnp.ones((DIM,), jnp.float32)
        be2 = jnp.zeros((DIM,), jnp.float32)
        return {'x': x, 'adj': adj, 'w_qkv': w_qkv, 'w_proj': w_proj, 'b_proj': b_proj, 'w1': w1, 'b1': b1, 'w2': w2, 'b2': b2, 'g1': g1, 'be1': be1, 'g2': g2, 'be2': be2}
    _L2_gnn_all = _L2_gnn_setup()
    _L2_gnn_in = {k: v for k, v in _L2_gnn_all.items() if k in ('w_qkv', 'w_proj', 'b_proj', 'w1', 'b1', 'w2', 'b2', 'g1', 'be1', 'g2', 'be2', )}
    del _L2_gnn_all

    def _L3_gnn_setup():
        import jax, jax.numpy as jnp
        import numpy as np
        DIM = 256
        HEADS = 8
        DIM_FF = 1024
        N = 4096
        HEAD_DIM = DIM // HEADS
        SCALE = HEAD_DIM ** (-0.5)

        def layer_norm(x, gamma, beta, eps=1e-05):
            mu = jnp.mean(x, axis=-1, keepdims=True)
            var = jnp.var(x, axis=-1, keepdims=True)
            return (x - mu) * jax.lax.rsqrt(var + eps) * gamma + beta
        key = jax.random.key(seed)
        ks = jax.random.split(key, 8)
        x = jax.random.normal(ks[0], (N, DIM), dtype=jnp.float32)
        adj = jax.random.randint(ks[1], (N, N), 0, 2, dtype=jnp.int32)
        adj = adj.at[jnp.arange(N), jnp.arange(N)].set(1)
        s = 1.0 / np.sqrt(DIM)
        w_qkv = jax.random.normal(ks[2], (DIM, 3 * DIM), dtype=jnp.float32) * s
        w_proj = jax.random.normal(ks[3], (DIM, DIM), dtype=jnp.float32) * s
        b_proj = jnp.zeros((DIM,), jnp.float32)
        w1 = jax.random.normal(ks[4], (DIM, DIM_FF), dtype=jnp.float32) * s
        b1 = jnp.zeros((DIM_FF,), jnp.float32)
        w2 = jax.random.normal(ks[5], (DIM_FF, DIM), dtype=jnp.float32) / np.sqrt(DIM_FF)
        b2 = jnp.zeros((DIM,), jnp.float32)
        g1 = jnp.ones((DIM,), jnp.float32)
        be1 = jnp.zeros((DIM,), jnp.float32)
        g2 = jnp.ones((DIM,), jnp.float32)
        be2 = jnp.zeros((DIM,), jnp.float32)
        return {'x': x, 'adj': adj, 'w_qkv': w_qkv, 'w_proj': w_proj, 'b_proj': b_proj, 'w1': w1, 'b1': b1, 'w2': w2, 'b2': b2, 'g1': g1, 'be1': be1, 'g2': g2, 'be2': be2}
    _L3_gnn_all = _L3_gnn_setup()
    _L3_gnn_in = {k: v for k, v in _L3_gnn_all.items() if k in ('w_qkv', 'w_proj', 'b_proj', 'w1', 'b1', 'w2', 'b2', 'g1', 'be1', 'g2', 'be2', )}
    del _L3_gnn_all

    return {
        "x": x,
        "adj": adj,
        "L0_gnn_w_qkv": _L0_gnn_in["w_qkv"],
        "L0_gnn_w_proj": _L0_gnn_in["w_proj"],
        "L0_gnn_b_proj": _L0_gnn_in["b_proj"],
        "L0_gnn_w1": _L0_gnn_in["w1"],
        "L0_gnn_b1": _L0_gnn_in["b1"],
        "L0_gnn_w2": _L0_gnn_in["w2"],
        "L0_gnn_b2": _L0_gnn_in["b2"],
        "L0_gnn_g1": _L0_gnn_in["g1"],
        "L0_gnn_be1": _L0_gnn_in["be1"],
        "L0_gnn_g2": _L0_gnn_in["g2"],
        "L0_gnn_be2": _L0_gnn_in["be2"],
        "L1_gnn_Wt": _L1_gnn_in["Wt"],
        "L1_gnn_bt": _L1_gnn_in["bt"],
        "L1_gnn_Wa": _L1_gnn_in["Wa"],
        "L1_gnn_ba": _L1_gnn_in["ba"],
        "L1_gnn_Wp": _L1_gnn_in["Wp"],
        "L1_gnn_bp": _L1_gnn_in["bp"],
        "L1_gnn_gamma": _L1_gnn_in["gamma"],
        "L1_gnn_beta": _L1_gnn_in["beta"],
        "L2_gnn_w_qkv": _L2_gnn_in["w_qkv"],
        "L2_gnn_w_proj": _L2_gnn_in["w_proj"],
        "L2_gnn_b_proj": _L2_gnn_in["b_proj"],
        "L2_gnn_w1": _L2_gnn_in["w1"],
        "L2_gnn_b1": _L2_gnn_in["b1"],
        "L2_gnn_w2": _L2_gnn_in["w2"],
        "L2_gnn_b2": _L2_gnn_in["b2"],
        "L2_gnn_g1": _L2_gnn_in["g1"],
        "L2_gnn_be1": _L2_gnn_in["be1"],
        "L2_gnn_g2": _L2_gnn_in["g2"],
        "L2_gnn_be2": _L2_gnn_in["be2"],
        "L3_gnn_w_qkv": _L3_gnn_in["w_qkv"],
        "L3_gnn_w_proj": _L3_gnn_in["w_proj"],
        "L3_gnn_b_proj": _L3_gnn_in["b_proj"],
        "L3_gnn_w1": _L3_gnn_in["w1"],
        "L3_gnn_b1": _L3_gnn_in["b1"],
        "L3_gnn_w2": _L3_gnn_in["w2"],
        "L3_gnn_b2": _L3_gnn_in["b2"],
        "L3_gnn_g1": _L3_gnn_in["g1"],
        "L3_gnn_be1": _L3_gnn_in["be1"],
        "L3_gnn_g2": _L3_gnn_in["g2"],
        "L3_gnn_be2": _L3_gnn_in["be2"],
    }

def reference(x, adj, L0_gnn_w_qkv, L0_gnn_w_proj, L0_gnn_b_proj, L0_gnn_w1, L0_gnn_b1, L0_gnn_w2, L0_gnn_b2, L0_gnn_g1, L0_gnn_be1, L0_gnn_g2, L0_gnn_be2, L1_gnn_Wt, L1_gnn_bt, L1_gnn_Wa, L1_gnn_ba, L1_gnn_Wp, L1_gnn_bp, L1_gnn_gamma, L1_gnn_beta, L2_gnn_w_qkv, L2_gnn_w_proj, L2_gnn_b_proj, L2_gnn_w1, L2_gnn_b1, L2_gnn_w2, L2_gnn_b2, L2_gnn_g1, L2_gnn_be1, L2_gnn_g2, L2_gnn_be2, L3_gnn_w_qkv, L3_gnn_w_proj, L3_gnn_b_proj, L3_gnn_w1, L3_gnn_b1, L3_gnn_w2, L3_gnn_b2, L3_gnn_g1, L3_gnn_be1, L3_gnn_g2, L3_gnn_be2):
    import jax
    import jax.numpy as jnp
    def _L0_gnn_ref(x, adj, w_qkv, w_proj, b_proj, w1, b1, w2, b2, g1, be1, g2, be2):
        import jax, jax.numpy as jnp
        import numpy as np
        DIM = 256
        HEADS = 8
        DIM_FF = 1024
        N = 4096
        HEAD_DIM = DIM // HEADS
        SCALE = HEAD_DIM ** (-0.5)

        def layer_norm(x, gamma, beta, eps=1e-05):
            mu = jnp.mean(x, axis=-1, keepdims=True)
            var = jnp.var(x, axis=-1, keepdims=True)
            return (x - mu) * jax.lax.rsqrt(var + eps) * gamma + beta
        n = x.shape[0]
        qkv = layer_norm(x, g1, be1) @ w_qkv
        qkv = qkv.reshape(n, 3, HEADS, HEAD_DIM)
        q, k, v = (qkv[:, 0], qkv[:, 1], qkv[:, 2])
        scores = jnp.einsum('nhd,mhd->hnm', q, k) * SCALE
        mask = (adj != 0)[None, :, :]
        scores = jnp.where(mask, scores, -jnp.inf)
        attn = jax.nn.softmax(scores, axis=-1)
        out = jnp.einsum('hnm,mhd->nhd', attn, v).reshape(n, DIM)
        x = x + out @ w_proj + b_proj
        h2 = layer_norm(x, g2, be2)
        ff = jax.nn.gelu(h2 @ w1 + b1) @ w2 + b2
        return x + ff

    def _L1_gnn_ref(x, adj, Wt, bt, Wa, ba, Wp, bp, gamma, beta):
        import jax, jax.numpy as jnp
        import numpy as np
        N = 8192
        F = 256
        H = 64
        NEG = -9000000000000000.0
        EPS = 1e-05
        h = x @ Wt.T + bt
        s = jax.nn.leaky_relu(h @ Wa.T + ba, negative_slope=0.2)
        scores = jnp.where(adj > 0, s, jnp.float32(NEG))
        w = jax.nn.softmax(scores, axis=1)
        neighbor = w @ h
        tf = neighbor @ Wp.T + bp
        y = x + tf
        mu = jnp.mean(y, axis=-1, keepdims=True)
        var = jnp.var(y, axis=-1, keepdims=True)
        return gamma * (y - mu) * jax.lax.rsqrt(var + EPS) + beta

    def _L2_gnn_ref(x, adj, w_qkv, w_proj, b_proj, w1, b1, w2, b2, g1, be1, g2, be2):
        import jax, jax.numpy as jnp
        import numpy as np
        DIM = 256
        HEADS = 8
        DIM_FF = 1024
        N = 4096
        HEAD_DIM = DIM // HEADS
        SCALE = HEAD_DIM ** (-0.5)

        def layer_norm(x, gamma, beta, eps=1e-05):
            mu = jnp.mean(x, axis=-1, keepdims=True)
            var = jnp.var(x, axis=-1, keepdims=True)
            return (x - mu) * jax.lax.rsqrt(var + eps) * gamma + beta
        n = x.shape[0]
        qkv = layer_norm(x, g1, be1) @ w_qkv
        qkv = qkv.reshape(n, 3, HEADS, HEAD_DIM)
        q, k, v = (qkv[:, 0], qkv[:, 1], qkv[:, 2])
        scores = jnp.einsum('nhd,mhd->hnm', q, k) * SCALE
        mask = (adj != 0)[None, :, :]
        scores = jnp.where(mask, scores, -jnp.inf)
        attn = jax.nn.softmax(scores, axis=-1)
        out = jnp.einsum('hnm,mhd->nhd', attn, v).reshape(n, DIM)
        x = x + out @ w_proj + b_proj
        h2 = layer_norm(x, g2, be2)
        ff = jax.nn.gelu(h2 @ w1 + b1) @ w2 + b2
        return x + ff

    def _L3_gnn_ref(x, adj, w_qkv, w_proj, b_proj, w1, b1, w2, b2, g1, be1, g2, be2):
        import jax, jax.numpy as jnp
        import numpy as np
        DIM = 256
        HEADS = 8
        DIM_FF = 1024
        N = 4096
        HEAD_DIM = DIM // HEADS
        SCALE = HEAD_DIM ** (-0.5)

        def layer_norm(x, gamma, beta, eps=1e-05):
            mu = jnp.mean(x, axis=-1, keepdims=True)
            var = jnp.var(x, axis=-1, keepdims=True)
            return (x - mu) * jax.lax.rsqrt(var + eps) * gamma + beta
        n = x.shape[0]
        qkv = layer_norm(x, g1, be1) @ w_qkv
        qkv = qkv.reshape(n, 3, HEADS, HEAD_DIM)
        q, k, v = (qkv[:, 0], qkv[:, 1], qkv[:, 2])
        scores = jnp.einsum('nhd,mhd->hnm', q, k) * SCALE
        mask = (adj != 0)[None, :, :]
        scores = jnp.where(mask, scores, -jnp.inf)
        attn = jax.nn.softmax(scores, axis=-1)
        out = jnp.einsum('hnm,mhd->nhd', attn, v).reshape(n, DIM)
        x = x + out @ w_proj + b_proj
        h2 = layer_norm(x, g2, be2)
        ff = jax.nn.gelu(h2 @ w1 + b1) @ w2 + b2
        return x + ff

    x = _L0_gnn_ref(x, adj, L0_gnn_w_qkv, L0_gnn_w_proj, L0_gnn_b_proj, L0_gnn_w1, L0_gnn_b1, L0_gnn_w2, L0_gnn_b2, L0_gnn_g1, L0_gnn_be1, L0_gnn_g2, L0_gnn_be2)
    x = _L1_gnn_ref(x, adj, L1_gnn_Wt, L1_gnn_bt, L1_gnn_Wa, L1_gnn_ba, L1_gnn_Wp, L1_gnn_bp, L1_gnn_gamma, L1_gnn_beta)
    x = _L2_gnn_ref(x, adj, L2_gnn_w_qkv, L2_gnn_w_proj, L2_gnn_b_proj, L2_gnn_w1, L2_gnn_b1, L2_gnn_w2, L2_gnn_b2, L2_gnn_g1, L2_gnn_be1, L2_gnn_g2, L2_gnn_be2)
    x = _L3_gnn_ref(x, adj, L3_gnn_w_qkv, L3_gnn_w_proj, L3_gnn_b_proj, L3_gnn_w1, L3_gnn_b1, L3_gnn_w2, L3_gnn_b2, L3_gnn_g1, L3_gnn_be1, L3_gnn_g2, L3_gnn_be2)
    return x


_drawn_inputs = setup_inputs


def setup_inputs(seed=0):
    import zlib

    import numpy as np

    out = dict(_drawn_inputs(seed))
    spreads = {'L0_gnn_b_proj': (0.0, 0.1),
     'L0_gnn_b1': (0.0, 0.1),
     'L0_gnn_b2': (0.0, 0.1),
     'L0_gnn_g1': (1.0, 0.2),
     'L0_gnn_be1': (0.0, 0.1),
     'L0_gnn_g2': (1.0, 0.2),
     'L0_gnn_be2': (0.0, 0.1),
     'L1_gnn_bt': (0.0, 0.1),
     'L1_gnn_bp': (0.0, 0.1),
     'L1_gnn_gamma': (1.0, 0.2),
     'L1_gnn_beta': (0.0, 0.1),
     'L2_gnn_b_proj': (0.0, 0.1),
     'L2_gnn_b1': (0.0, 0.1),
     'L2_gnn_b2': (0.0, 0.1),
     'L2_gnn_g1': (1.0, 0.2),
     'L2_gnn_be1': (0.0, 0.1),
     'L2_gnn_g2': (1.0, 0.2),
     'L2_gnn_be2': (0.0, 0.1),
     'L3_gnn_b_proj': (0.0, 0.1),
     'L3_gnn_b1': (0.0, 0.1),
     'L3_gnn_b2': (0.0, 0.1),
     'L3_gnn_g1': (1.0, 0.2),
     'L3_gnn_be1': (0.0, 0.1),
     'L3_gnn_g2': (1.0, 0.2),
     'L3_gnn_be2': (0.0, 0.27)}
    factors = {}
    for name, (base, spread) in spreads.items():
        noise = np.random.default_rng([zlib.crc32(name.encode()), seed]).standard_normal(out[name].shape)
        drawn = base * np.exp(spread * noise) if base else spread * noise
        out[name] = jnp.asarray(drawn.astype(out[name].dtype))
    for name, factor in factors.items():
        out[name] = (out[name] * factor).astype(out[name].dtype)
    return out
```

```python
from contextlib import ExitStack

import numpy as np

import concourse.bass as bass
from concourse import mybir

ALU = mybir.AluOpType
ACT = mybir.ActivationFunctionType
F32 = mybir.dt.float32
BF16 = mybir.dt.bfloat16
F8 = mybir.dt.float8e4
I32 = mybir.dt.int32
U32 = mybir.dt.uint32
AX_X = mybir.AxisListType.X
RMAX = bass.bass_isa.ReduceOp.max

P = 128
HEADS = 8
GROUP = 4
EPS = 1e-5
NEG = -9e15
MASKED = -1e30
RSQRT_MAGIC = float(0x5F3759DF)
GELU_CUBE = 0.044715
GELU_SCALE = 0.7978845608028654


class Counter:

    def __init__(self, sem):
        self.sem, self.value = sem, 0

    def up(self, by):
        self.value += by
        return (self, self.value)


class Queues:

    def __init__(self, ends):
        self.ends = ends
        self.steps = {k: [] for k in ("sync", "pe", "dve", "act", "pool")}

    def put(self, engine, waits, make, counter=None, by=1):
        mark = counter.up(by) if counter is not None else None
        self.steps[engine].append(([w for w in waits if w is not None], make, counter, by))
        return mark

    def pe(self, make, *waits, end=True):
        return self.put("pe", waits, make, self.ends["pe"] if end else None)

    def dve(self, make, *waits):
        return self.put("dve", waits, make, self.ends["dve"])

    def act(self, make, *waits):
        return self.put("act", waits, make, self.ends["act"])

    def pool(self, make, *waits):
        return self.put("pool", waits, make, self.ends["pool"])

    def load(self, out, in_, landed, *waits, engine="sync"):
        return self.put(engine, waits, lambda e: e.dma_start(out, in_), landed, 16)

    def emit(self, block):
        for name, on in (("sync", block.sync), ("pe", block.tensor), ("dve", block.vector),
                         ("act", block.scalar), ("pool", block.gpsimd)):
            def program(e, steps=self.steps[name]):
                passed = {}
                for waits, make, counter, by in steps:
                    for c, value in waits:
                        if passed.get(id(c), 0) < value:
                            e.wait_ge(c.sem, value)
                            passed[id(c)] = value
                    ins = make(e)
                    if counter is not None:
                        ins.then_inc(counter.sem, by)
            on(program)
            self.steps[name] = []


def graph_layers(nc, x_d, adj_d, layers_d, gat_d, out_d, n_real):
    NP, D = x_d.shape
    T = NP // P
    PAIRS = T // 2
    HD = D // HEADS
    KD = D // P
    FF = layers_d[0]["w1"].shape[1]
    KF = FF // P
    GH = gat_d["wt"].shape[1]
    SCALE = float(HD) ** -0.5
    GW = 3 * GH + 1

    kv_d = [nc.dram_tensor(f"kv_rows_{i}", [NP, 2 * D], F32).ap() for i in range(2)]
    adjT_d = nc.dram_tensor("adj_transposed", [T, P, NP], F8).ap()
    att_d = nc.dram_tensor("dense_attention_out", [NP, D], F32).ap()

    with ExitStack() as top:
        def sem(n):
            return top.enter_context(nc.semaphore(n))

        times = {}

        def sbuf(n, shape, dt=F32, where=top):
            times[n] = times.get(n, 0) + 1
            n += f"_{times[n]}" if times[n] > 1 else ""
            return where.enter_context(nc.sbuf_tensor(n, shape, dt))

        x = sbuf("x_nodes", [P, T, D])
        q_parts = sbuf("q_parts", [P, T, 3, D], BF16)
        identf = sbuf("identity_f32", [P, P])
        identb = sbuf("identity_bf16", [P, P], BF16)
        w_qkv = sbuf("w_qkv", [P, KD, 3 * D])
        w_proj = sbuf("w_proj", [P, KD, D])
        w_1 = sbuf("w_1", [P, KD, FF])
        w_2 = sbuf("w_2", [P, KF, D])
        cols = sbuf("bias_and_norm_columns", [P, KF + 4 * KD])
        rows = sbuf("bias_rows", [P, 2, D])
        att = sbuf("attention_pair", [P, 2, 2, D])
        attT = sbuf("attention_transposed", [P, KD, 2 * P])
        xn = sbuf("normalised", [P, 2, D])
        h2T = sbuf("ff_input_transposed", [P, KD, 2 * P])
        h1T = sbuf("qkv_input_transposed", [P, KD, 2 * P])
        ffh = sbuf("ff_hidden", [P, KF, 2 * P])
        ffu = sbuf("ff_gelu_argument", [P, KF, 2 * P])
        xb1 = sbuf("x_plus_b_proj", [P, 2, D])
        xb2 = sbuf("x_plus_b2", [P, 2, D])
        kv_st = sbuf("kv_to_store", [P, 2, 2 * D])
        q_rest = sbuf("q_rest", [P, 2, D])
        stat = sbuf("norm_statistics", [P, 2, 6])
        mv = sbuf("mean_and_variance", [P, 2, 2])
        nw = sbuf("rsqrt_work", [P, 6, 2])
        gh = sbuf("h_parts_and_one", [P, T, GW], BF16)
        gs = sbuf("gat_row_scores", [P, T])

        psum = lambda n, shape: top.enter_context(nc.psum_tensor(n, shape, F32))
        ps_q = psum("ps_q", [P, 2, 512])
        ps_a = psum("ps_a", [P, 512])
        ps_t = psum("ps_t", [P, 512])
        ps_w = psum("ps_w", [P, 2, 512])
        ps_o = psum("ps_o", [P, 2, 512])

        ends = {k: Counter(sem("steps_done_" + k)) for k in ("pe", "dve", "act", "pool")}
        loop_ends = {k: sem("dense_steps_done_" + k) for k in ("pe", "dve", "act", "pool")}
        loop_dma = [sem(f"dense_loaded_{i}") for i in range(3)]
        loop_sems = range(loop_ends["pe"].num, loop_dma[-1].num + 1)
        s_w = Counter(sem("weights_landed"))
        s_w2 = Counter(sem("qkv_weights_landed"))
        s_x = Counter(sem("x_landed"))
        s_adj = [Counter(sem(f"adj_landed_{i}")) for i in range(2)]
        s_at = [Counter(sem(f"adj_transposed_moved_{i}")) for i in range(3)]
        s_kv = [Counter(sem(f"kv_stored_{i}")) for i in range(2)]
        s_ad = [Counter(sem(f"dense_attention_landed_{i}")) for i in range(2)]
        s_out = Counter(sem("out_stored"))
        Q = Queues(ends)
        last = {}

        cb1, cg2, cbe2, cg1, cbe1 = 0, KF, KF + KD, KF + 2 * KD, KF + 3 * KD

        def load_main_weights(L):
            d = layers_d[L]
            Q.load(w_proj[:], d["w_proj"].rearrange("(k p) n -> p k n", p=P), s_w)
            Q.load(cols[:, 0:cg1], d["cols"][:, 0:cg1], s_w)
            Q.load(rows[:], d["rows"], s_w)
            Q.load(w_1[:], d["w1"].rearrange("(k p) n -> p k n", p=P), s_w)
            return Q.load(w_2[:], d["w2"].rearrange("(k p) n -> p k n", p=P), s_w)

        def load_qkv_weights(L):
            d = layers_d[L]
            Q.load(cols[:, cg1:], d["cols"][:, cg1:], s_w2)
            return Q.load(w_qkv[:], d["w_qkv"].rearrange("(k p) n -> p k n", p=P), s_w2)

        def normalise(src, ready):
            m = ready
            for i in range(2):
                m = Q.dve(lambda e, i=i: e.bn_stats(stat[:, i, :], src[:, i, :]), ready)
            for i in range(2):
                m = Q.dve(lambda e, i=i: e.bn_aggr(mv[:, i, :], stat[:, i, :]), m)
            var = mv[:, :, 1]
            v, hv, y, a, sh = (nw[:, j, :] for j in range(5))
            Q.dve(lambda e: e.tensor_scalar(v, var, EPS, None, ALU.add), m)
            m = Q.dve(lambda e: e.tensor_scalar(hv, var, EPS, -0.5, ALU.add, ALU.mult), m)
            m = Q.dve(lambda e: e.tensor_scalar(sh.bitcast(I32), v.bitcast(I32), 1, None, ALU.logical_shift_right), m)
            m = Q.dve(lambda e: e.tensor_scalar(y.bitcast(I32), sh.bitcast(I32), -1.0, RSQRT_MAGIC, ALU.mult, ALU.add), m)
            for _ in range(3):
                m = Q.dve(lambda e: e.tensor_tensor(a, y, y, ALU.mult), m)
                m = Q.dve(lambda e: e.tensor_tensor(a, a, hv, ALU.mult), m)
                m = Q.dve(lambda e: e.scalar_tensor_tensor(out=y, in0=a, scalar=1.5, in1=y, op0=ALU.add, op1=ALU.mult), m)
            for i in range(2):
                w = Q.dve(lambda e, i=i: e.tensor_scalar(xn[:, i, :], src[:, i, :], mv[:, i, 0:1], y[:, i:i + 1],
                                                         ALU.subtract, ALU.mult), m, last.get("xn"))
            return w

        def transpose_pair(src, ready, width=D):
            for k in range(KD):
                for i in range(2):
                    o = (2 * k + i) * P
                    m = Q.pe(lambda e, k=k, i=i, o=o: e.transpose(ps_t[:, o:o + P], src[:, i, k * P:(k + 1) * P], identf[:]),
                             ready, last.get("ps_t"), end=(k, i) == (KD - 1, 1))
            return m

        def scaled_out(dst, name, g_col, b_col, turned, ready):
            for k in range(KD):
                m = Q.act(lambda e, k=k: e.activation(dst[:, k, :], ps_t[:, k * 2 * P:(k + 1) * 2 * P], ACT.Identity,
                                                      bias=cols[:, b_col + k:b_col + k + 1],
                                                      scale=cols[:, g_col + k:g_col + k + 1]),
                          turned, last.get(name), ready)
            last["ps_t"] = m
            return m

        def qkv_stages(g, table, after, qkv_w):
            s = {}

            def norm():
                s["n"] = normalise(x[:, 2 * g:2 * g + 2, :], after())

            def turn():
                t = transpose_pair(xn, s["n"])
                last["xn"] = t
                s["h"] = scaled_out(h1T, "h1T", cg1, cbe1, t, qkv_w)

            def tile(i):
                t = 2 * g + i
                for c0, c1 in ((0, 512), (512, 768)):
                    for k in range(KD):
                        m = Q.pe(lambda e, i=i, k=k, c0=c0, c1=c1: e.matmul(
                            ps_o[:, c0 // 512, 0:c1 - c0], h1T[:, k, i * P:(i + 1) * P], w_qkv[:, k, c0:c1],
                            start=(k == 0), stop=(k == KD - 1)), s["h"], qkv_w, last.get("ps_o0"), last.get("ps_o1"),
                            end=(c0 and k == KD - 1))
                last["h1T"] = m
                qh, qm, ql = (q_parts[:, t, j, :] for j in range(3))
                a1 = Q.act(lambda e: e.activation(qh, ps_o[:, 0, 0:D], ACT.Copy), m, last.get(("q", t)))
                a2 = Q.act(lambda e: e.activation(kv_st[:, i, 0:D], ps_o[:, 0, D:2 * D], ACT.Copy), m, last.get(("kv_st", i)))
                a3 = Q.act(lambda e: e.activation(kv_st[:, i, D:2 * D], ps_o[:, 1, 0:D], ACT.Copy), m)
                d1 = Q.dve(lambda e: e.tensor_tensor(q_rest[:, i, :], ps_o[:, 0, 0:D], qh, ALU.subtract), a2, m,
                           last.get(("q_rest", i)))
                p1 = Q.pool(lambda e: e.tensor_copy(qm, q_rest[:, i, :]), d1)
                p2 = Q.pool(lambda e: e.tensor_tensor(ql, q_rest[:, i, :], qm, ALU.subtract), p1)
                last[("q_rest", i)] = p2
                last["ps_o0"], last["ps_o1"] = d1, a3
                last[("kv_st", i)] = Q.load(kv_d[table][t * P:(t + 1) * P, :], kv_st[:, i, :], s_kv[i], a2, a3)

            return [norm, turn, lambda: tile(0), lambda: tile(1)]

        def gat_input_stages(g, after, gw):
            s = {}

            def turn():
                t = transpose_pair(x[:, 2 * g:2 * g + 2, :], after())
                s["h"] = Q.act(lambda e: e.activation(h1T[:].rearrange("p k n -> p (k n)"), ps_t[:], ACT.Copy), t, last.get("h1T"))
                last["ps_t"] = s["h"]

            def tile(i):
                t = 2 * g + i
                for k in range(KD):
                    m = Q.pe(lambda e, k=k: e.matmul(ps_o[:, 0, 0:GH], h1T[:, k, i * P:(i + 1) * P], g_wt[:, k, :],
                                                     start=(k == 0), stop=(k == KD - 1)), s["h"], gw, last.get("ps_o0"),
                             end=k == KD - 1)
                last["h1T"] = m
                hf = g_work[:, i, 0:GH]
                hr = g_work[:, i, GH:2 * GH]
                hw = g_work[:, i, 2 * GH:3 * GH]
                d = Q.dve(lambda e: e.tensor_tensor(hf, ps_o[:, 0, 0:GH], g_rows[:, 0:GH], ALU.add), m, gw, last.get(("gw", i)))
                last["ps_o0"] = d
                a = Q.dve(lambda e: e.tensor_tensor_reduce(hw, hf, g_rows[:, GH:2 * GH], 1.0, 0.0, ALU.mult, ALU.add,
                                                           gs[:, t:t + 1]), d)
                p = Q.pool(lambda e: e.tensor_copy(gh[:, t, 0:GH], hf), d)
                p = Q.pool(lambda e: e.tensor_tensor(hr, hf, gh[:, t, 0:GH], ALU.subtract), p, d)
                p = Q.pool(lambda e: e.tensor_copy(gh[:, t, GH:2 * GH], hr), p)
                p = Q.pool(lambda e: e.tensor_tensor(gh[:, t, 2 * GH:3 * GH], hr, gh[:, t, GH:2 * GH], ALU.subtract), p)
                last[("gw", i)] = p
                last["gs"] = a
                last["gh"] = p

            return [turn, lambda: tile(0), lambda: tile(1)]

        def mlp_stages(g, att_ready, wts, then):
            s = {}
            b = g % 2
            xp = x[:, 2 * g:2 * g + 2, :]
            row = lambda j: rows[:, j, :].unsqueeze(1).to_broadcast([P, 2, D])

            def project():
                t = transpose_pair(att[:, b], att_ready())
                last[("att", b)] = t
                a = Q.act(lambda e: e.activation(attT[:].rearrange("p k n -> p (k n)"), ps_t[:], ACT.Copy), t, last.get("attT"))
                last["ps_t"] = a
                p = Q.pool(lambda e: e.tensor_tensor(xb1[:], xp, row(0), ALU.add), wts, last.get("xb1"), last.get("x"))
                for i in range(2):
                    for k in range(KD):
                        m = Q.pe(lambda e, i=i, k=k: e.matmul(ps_o[:, 0, i * D:(i + 1) * D], attT[:, k, i * P:(i + 1) * P],
                                                              w_proj[:, k, :], start=(k == 0), stop=(k == KD - 1)),
                                 a, wts, last.get("ps_o0"), end=(i == 1 and k == KD - 1))
                last["attT"] = m
                d = Q.dve(lambda e: e.tensor_tensor(xp, ps_o[:, 0, :].rearrange("p (i n) -> p i n", i=2), xb1[:], ALU.add), m, p)
                last["ps_o0"] = last["xb1"] = d
                s["x1"] = d
                s["xb2"] = Q.pool(lambda e: e.tensor_tensor(xb2[:], xp, row(1), ALU.add), d, last.get("xb2"))

            def norm():
                s["n"] = normalise(xp, s["x1"])

            def turn():
                t = transpose_pair(xn, s["n"])
                last["xn"] = t
                s["h"] = scaled_out(h2T, "h2T", cg2, cbe2, t, wts)

            def up(c):
                bank = c % 2
                for j in range(2):
                    f = 2 * c + j
                    for k in range(KD):
                        m = Q.pe(lambda e, j=j, f=f, k=k: e.matmul(ps_w[:, bank, j * 2 * P:(j + 1) * 2 * P],
                                                                   w_1[:, k, f * P:(f + 1) * P], h2T[:, k, :],
                                                                   start=(k == 0), stop=(k == KD - 1)),
                                 s["h"], wts, last.get(("ps_w", bank)), end=(j == 1 and k == KD - 1))
                last["h2T"] = m
                for j in range(2):
                    f = 2 * c + j
                    src = ps_w[:, bank, j * 2 * P:(j + 1) * 2 * P]
                    Q.act(lambda e, f=f, src=src: e.activation(ffh[:, f, :], src, ACT.Identity, bias=cols[:, cb1 + f:cb1 + f + 1]),
                          m, last.get(("ffh", f // 4)))
                    a = Q.act(lambda e, f=f, src=src: e.activation(ffu[:, f, :], src, ACT.Square, bias=cols[:, cb1 + f:cb1 + f + 1]),
                              m, last.get(("ffu", f // 4)))
                last[("ps_w", bank)] = a
                if c % 2:
                    half = c // 2
                    hh, uu = ffh[:, 4 * half:4 * half + 4, :], ffu[:, 4 * half:4 * half + 4, :]
                    p = Q.dve(lambda e: e.scalar_tensor_tensor(out=uu, in0=uu, scalar=1.0 / GELU_CUBE, in1=hh, op0=ALU.add,
                                                                op1=ALU.mult), a)
                    a = Q.act(lambda e: e.activation(uu, uu, ACT.Tanh, scale=GELU_SCALE * GELU_CUBE), p)
                    s[("g", half)] = Q.dve(lambda e: e.scalar_tensor_tensor(out=hh, in0=uu, scalar=1.0, in1=hh, op0=ALU.add,
                                                                            op1=ALU.mult), a)
                    last[("ffu", half)] = s[("g", half)]

            def down():
                for i in range(2):
                    for f in range(KF):
                        m = Q.pe(lambda e, i=i, f=f: e.matmul(ps_o[:, 1, i * D:(i + 1) * D], ffh[:, f, i * P:(i + 1) * P],
                                                              w_2[:, f, :], start=(f == 0), stop=(f == KF - 1)),
                                 s[("g", f // 4)], wts, last.get("ps_o1"), end=(i == 1 and f == KF - 1))
                last[("ffh", 0)] = last[("ffh", 1)] = m
                d = Q.dve(lambda e: e.scalar_tensor_tensor(out=xp, in0=ps_o[:, 1, :].rearrange("p (i n) -> p i n", i=2),
                                                           scalar=0.5, in1=xb2[:], op0=ALU.mult, op1=ALU.add), m, s["xb2"])
                last["ps_o1"] = last["xb2"] = d
                s["x2"] = d

            return [project, norm, turn, lambda: up(0), lambda: up(1), lambda: up(2), lambda: up(3), down] + then(lambda: s["x2"])

        def store_stage(g, after):
            def store():
                for i in range(2):
                    t = 2 * g + i
                    n = min(P, n_real - t * P)
                    last["out"] = Q.load(out_d[t * P:t * P + n, :], x[0:n, t, :], s_out, after())
            return [store]

        with ExitStack() as ph:
            adj_i = sbuf("adj_rows", [P, 2, NP], I32, ph)
            adj_b = sbuf("adj_rows_bf16", [P, 2, NP], BF16, ph)
            at_st = sbuf("adj_transposed_tile", [P, 2, NP], F8, ph)
            p1 = Q.pool(lambda e: e.memset(identf[:], 0.0))
            p1 = Q.pool(lambda e: e.affine_select(out=identf[:], in_=identf[:], compare_op=ALU.not_equal, fill=1.0, base=0,
                                                  pattern=[[-1, P]], channel_multiplier=1), p1)
            ident_ready = Q.pool(lambda e: e.tensor_copy(identb[:], identf[:]), p1)
            Q.pool(lambda e: e.memset(gh[:], 1.0))
            for g in range(PAIRS):
                xl = Q.load(x[:, 2 * g:2 * g + 2, :], x_d[2 * g * P:(2 * g + 2) * P, :].rearrange("(i p) d -> p i d", p=P), s_x)
                if g == 0:
                    qw = load_qkv_weights(0)
                elif g == 1:
                    load_main_weights(0)
            xl_all = xl

            def transpose_adj(t):
                b = t % 2
                landed = Q.load(adj_i[:, b, :], adj_d[t * P:(t + 1) * P, :], s_adj[b], last.get(("adj_i", b)))
                a = Q.act(lambda e: e.activation(adj_b[:, b, :], adj_i[:, b, :], ACT.Sign), landed, last.get(("adj_b", b)))
                last[("adj_i", b)] = a
                for n, m0 in enumerate(range(0, T, 8)):
                    bank = n % 2
                    view = ps_w[:, bank, :].bitcast(BF16)
                    cnt = min(8, T - m0)
                    for m in range(cnt):
                        tr = Q.pe(lambda e, m=m, m0=m0, view=view: e.transpose(
                            view[:, m * P:(m + 1) * P], adj_b[:, b, (m0 + m) * P:(m0 + m + 1) * P], identb[:]),
                            a, ident_ready, last.get(("ps_w", bank)), end=m == cnt - 1)
                    dst = at_st[:, b, m0 * P:(m0 + cnt) * P]
                    if n % 2:
                        c = Q.act(lambda e, dst=dst, view=view, cnt=cnt: e.activation(dst, view[:, 0:cnt * P], ACT.Copy, saturate=False),
                                  tr, last.get(("at_st", b)))
                    else:
                        c = Q.dve(lambda e, dst=dst, view=view, cnt=cnt: e.tensor_copy(dst, view[:, 0:cnt * P], saturate=False),
                                  tr, last.get(("at_st", b)))
                    last[("ps_w", bank)] = c
                last[("adj_b", b)] = tr
                last[("at_st", b)] = Q.load(adjT_d[t], at_st[:, b, :], s_at[b], last[("ps_w", 0)], last[("ps_w", 1)])

            for g in range(PAIRS):
                st = qkv_stages(g, 0, lambda: xl_all, qw)
                transpose_adj(2 * g)
                st[0](); st[1]()
                transpose_adj(2 * g + 1)
                st[2](); st[3]()
            finish(Q, nc, [s_x, s_w, s_w2] + s_adj + s_at + s_kv)
        last.clear()

        def dense_attention(table):
            S0, S1, S2 = (lambda: Counter(loop_dma[0])), (lambda: Counter(loop_dma[1])), (lambda: Counter(loop_dma[2]))
            with ExitStack() as ph:
                mask = sbuf("dense_mask", [P, NP], I32, ph)
                sc = sbuf("dense_scores", [P, NP], F32, ph)
                kT = sbuf("dense_keys_transposed", [P, NP], F32, ph)
                vg = sbuf("dense_values", [P, T, P], F32, ph)
                pT = sbuf("dense_weights_transposed", [P, 2, 512], F32, ph)
                qp = sbuf("dense_q_parts", [P, 3, P], BF16, ph)
                qT = sbuf("dense_q_transposed", [P, P], F32, ph)
                og = sbuf("dense_out_tile", [P, P], F32, ph)
                st = sbuf("dense_row_statistics", [P, 4], F32, ph)
                banks = [ps_q[:, 0, :], ps_q[:, 1, :], ps_a[:], ps_t[:], ps_w[:, 0, :], ps_w[:, 1, :], ps_o[:, 0, :]]
                maskf = mask[:].bitcast(F32)
                for grp in range(HEADS // GROUP):
                    c0 = grp * P
                    q = Queues({k: Counter(s) for k, s in loop_ends.items()})
                    s0, s1, s2 = S0(), S1(), S2()
                    kl = q.load(sc[:].rearrange("p (t c) -> p t c", c=P),
                                kv_d[table][:, c0:c0 + P].rearrange("(t p) c -> p t c", p=P), s0)
                    vl = q.load(vg[:], kv_d[table][:, D + c0:D + c0 + P].rearrange("(t p) c -> p t c", p=P), s1)
                    evac = None
                    for m0 in range(0, T, 4):
                        cnt = min(4, T - m0)
                        for m in range(cnt):
                            tr = q.pe(lambda e, m=m, m0=m0: e.transpose(ps_t[:, m * P:(m + 1) * P], sc[:, (m0 + m) * P:(m0 + m + 1) * P],
                                                                        identf[:]), kl, evac, end=m == cnt - 1)
                        evac = q.dve(lambda e, m0=m0, cnt=cnt: e.tensor_copy(kT[:, m0 * P:(m0 + cnt) * P], ps_t[:, 0:cnt * P]), tr)
                    with nc.Block() as block:
                        q.put("sync", [vl, evac], lambda e: e.nop())
                        q.emit(block)
                    nc.all_engine_barrier(sems_to_clear=loop_sems)
                    with nc.Fori(0, T) as it:
                        q = Queues({k: Counter(s) for k, s in loop_ends.items()})
                        s0, s1, s2 = S0(), S1(), S2()
                        ml = q.load(mask[:], adj_d[bass.ds(it * P, P), :], s0)
                        ql = q.load(qp[:], q_parts[:, bass.ds(it, 1), :, c0:c0 + P], s1)
                        mk = q.dve(lambda e: e.tensor_scalar(maskf, mask[:], 0, MASKED, ALU.is_equal, ALU.mult), ml)
                        for j in range(3):
                            m = q.pe(lambda e, j=j: e.matmul(ps_o[:, 1, 0:P], qp[:, j, :], identb[:], start=(j == 0), stop=(j == 2)),
                                     ql, end=j == 2)
                        qt = q.dve(lambda e: e.tensor_copy(qT[:], ps_o[:, 1, 0:P]), m)
                        freed = ov = None
                        for h in range(GROUP):
                            r0 = h * HD
                            for c in range(0, NP, 512):
                                w = min(512, NP - c)
                                m = q.pe(lambda e, c=c, w=w, r0=r0: e.matmul(banks[c // 512][:, 0:w], qT[r0:r0 + HD, :], kT[r0:r0 + HD, c:c + w],
                                                                             start=True, stop=True), qt, freed, end=c + w == NP)
                            d = None
                            for c in range(0, NP, 512):
                                w = min(512, NP - c)
                                d = q.dve(lambda e, c=c, w=w: e.tensor_tensor_reduce(
                                    sc[:, c:c + w], banks[c // 512][:, 0:w], maskf[:, c:c + w], 1.0,
                                    -3e38 if c == 0 else st[:, 0:1], ALU.add, ALU.max, st[:, 0:1]), m, mk, d, freed)
                            d = q.dve(lambda e: e.tensor_scalar(st[:, 1:2], st[:, 0:1], -SCALE, None, ALU.mult), d, freed)
                            a = q.act(lambda e: e.activation(sc[:], sc[:], ACT.Exp, bias=st[:, 1:2], scale=SCALE, accum_out=st[:, 2:3]), d)
                            rd = q.dve(lambda e: e.reciprocal(st[:, 3:4], st[:, 2:3]), a)
                            pv = [None, None]
                            for n, m0 in enumerate(range(0, T, 4)):
                                cnt = min(4, T - m0)
                                for m in range(cnt):
                                    tr = q.pe(lambda e, m=m, m0=m0, n=n: e.transpose(banks[n][:, m * P:(m + 1) * P],
                                                                                    sc[:, (m0 + m) * P:(m0 + m + 1) * P], identf[:]),
                                              a, d, end=m == cnt - 1)
                                ev = q.act(lambda e, n=n, cnt=cnt: e.activation(pT[:, n % 2, 0:cnt * P], banks[n][:, 0:cnt * P], ACT.Copy),
                                           tr, pv[n % 2])
                                for m in range(cnt):
                                    mm = q.pe(lambda e, m=m, m0=m0, n=n, r0=r0: e.matmul(
                                        ps_o[:, 1, 0:HD], pT[:, n % 2, m * P:(m + 1) * P], vg[:, m0 + m, r0:r0 + HD],
                                        start=(m0 + m == 0), stop=(m0 + m == T - 1)), ev, ov, qt, end=m == cnt - 1)
                                pv[n % 2] = mm
                            freed = ov = q.dve(lambda e, r0=r0: e.tensor_scalar(og[:, r0:r0 + HD], ps_o[:, 1, 0:HD], st[:, 3:4], None, ALU.mult),
                                               mm, rd)
                        done = q.load(att_d[bass.ds(it * P, P), c0:c0 + P], og[:], s2, ov)
                        q.put("sync", [done], lambda e: e.nop())
                        with nc.Block() as block:
                            q.emit(block)
                        nc.all_engine_barrier(sems_to_clear=loop_sems)

        def transformer_layer(L, table, next_table):
            dense_attention(table)
            if L > 0:
                wm = load_main_weights(L)
            else:
                wm = (s_w, s_w.value)
            qw = None
            if L == 1:
                qw = load_qkv_weights(2)
            if L == 0:
                gw = load_gat()
            for g in range(PAIRS):
                b = g % 2
                al = Q.load(att[:, b], att_d[2 * g * P:(2 * g + 2) * P, :].rearrange("(i p) d -> p i d", p=P), s_ad[b], last.get(("att", b)))
                if L == 0:
                    then = lambda x2, g=g: gat_input_stages(g, x2, gw)
                elif L == 1:
                    then = lambda x2, g=g: qkv_stages(g, next_table, x2, qw)
                else:
                    then = lambda x2, g=g: store_stage(g, x2)
                for f in mlp_stages(g, lambda al=al: al, wm, then):
                    f()
            finish(Q, nc, [s_w, s_w2, s_out] + s_kv + s_ad)
            last.clear()

        g_wt = sbuf("gat_wt", [P, KD, GH])
        g_wp = sbuf("gat_wp", [GH, D])
        g_rows = sbuf("gat_rows", [P, 2 * GH + 1 + 3 * D])
        g_work = sbuf("gat_work", [P, 2, 3 * GH])
        o_bp = 2 * GH + 1

        def load_gat():
            Q.load(g_wt[:], gat_d["wt"].rearrange("(k p) n -> p k n", p=P), s_w)
            Q.load(g_wp[:], gat_d["wp"], s_w)
            return Q.load(g_rows[:], gat_d["rows"], s_w)

        def gat_layer(next_table):
            qw = load_qkv_weights(1)
            with ExitStack() as ph:
                atb = sbuf("adj_transposed_in", [P, 3, NP], F8, ph)
                ga = sbuf("gat_sums", [P, 2, GW], F32, ph)
                ones = sbuf("ones", [P, P], BF16, ph)
                ef = sbuf("gat_row_weights", [P, 6, T], F32, ph)
                htot = sbuf("h_total", [P, 3 * GH], F32, ph)
                hsum = sbuf("h_total_sum", [P, GH], F32, ph)
                nb = sbuf("neighbour_mean", [P, 2, GH], F32, ph)
                dn = sbuf("gat_denominator", [P, 2, 2], F32, ph)
                nbT = sbuf("neighbour_transposed", [GH, 2 * P], F32, ph)
                xbp = sbuf("x_plus_bp", [P, 2, D], F32, ph)
                on = Q.pool(lambda e: e.memset(ones[:], 1.0))
                for t in range(T):
                    n = min(P, n_real - t * P)
                    m = Q.pe(lambda e, t=t, n=n: e.matmul(ps_a[:, 0:3 * GH], ones[0:n, :], gh[0:n, t, 0:3 * GH],
                                                          start=(t == 0), stop=(t == T - 1)), on, end=t == T - 1)
                a = Q.act(lambda e: e.activation(htot[:], ps_a[:, 0:3 * GH], ACT.Copy), m)
                d = Q.dve(lambda e: e.tensor_tensor(hsum[:], htot[:, 0:GH], htot[:, GH:2 * GH], ALU.add), a)
                hs = Q.dve(lambda e: e.tensor_tensor(hsum[:], hsum[:], htot[:, 2 * GH:3 * GH], ALU.add), d)
                s_, mx, ee, ff, dif, fn = (ef[:, j, :] for j in range(6))
                d = Q.dve(lambda e: e.tensor_scalar(mx, gs[:], g_rows[:, 2 * GH:2 * GH + 1], None, ALU.add))
                d = Q.dve(lambda e: e.scalar_tensor_tensor(out=s_, in0=mx, scalar=0.2, in1=mx, op0=ALU.mult, op1=ALU.max), d)
                d = Q.dve(lambda e: e.tensor_scalar(mx, s_, NEG, None, ALU.max), d)
                d1 = Q.dve(lambda e: e.tensor_tensor(ee, s_, mx, ALU.subtract), d)
                d2 = Q.dve(lambda e: e.tensor_scalar(ff, mx, -1.0, NEG, ALU.mult, ALU.add), d)
                a1 = Q.act(lambda e: e.activation(ef[:, 2:4, :], ef[:, 2:4, :], ACT.Exp), d2)
                d = Q.dve(lambda e: e.tensor_tensor(dif, ee, ff, ALU.subtract), a1)
                rw = Q.dve(lambda e: e.tensor_scalar(fn, ff, float(n_real), None, ALU.mult), d)

                def aggregate(t):
                    b = t % 3
                    al = Q.load(atb[:, b, :], adjT_d[t], s_at[b], last.get(("atb", b)))
                    for m0 in range(T):
                        m = Q.pe(lambda e, m0=m0: e.matmul(ps_q[:, t % 2, 0:GW], atb[:, b, m0 * P:(m0 + 1) * P], gh[:, m0, :],
                                                           start=(m0 == 0), stop=(m0 == T - 1)), al, last.get(("ps_q", t % 2)),
                                 end=m0 == T - 1)
                    last[("atb", b)] = m
                    return m

                def rest(g, sums):
                    xp = x[:, 2 * g:2 * g + 2, :]
                    row = lambda j: g_rows[:, o_bp + j * D:o_bp + (j + 1) * D].unsqueeze(1).to_broadcast([P, 2, D])
                    s = {}

                    def mean_of(i):
                        t = 2 * g + i
                        G = lambda j: ga[:, i, j * GH:(j + 1) * GH]
                        a = Q.act(lambda e: e.activation(ga[:, i, :], ps_q[:, i, 0:GW], ACT.Copy), sums[i], last.get(("ga", i)))
                        last[("ps_q", i)] = a
                        d = Q.dve(lambda e: e.tensor_tensor(G(0), G(0), G(1), ALU.add), a)
                        d = Q.dve(lambda e: e.tensor_tensor(G(0), G(0), G(2), ALU.add), d)
                        d = Q.dve(lambda e: e.tensor_scalar(G(0), G(0), dif[:, t:t + 1], None, ALU.mult), d, rw)
                        d = Q.dve(lambda e: e.scalar_tensor_tensor(out=G(1), in0=hsum[:], scalar=ff[:, t:t + 1], in1=G(0),
                                                                   op0=ALU.mult, op1=ALU.add), d, hs)
                        c = Q.dve(lambda e: e.tensor_scalar(dn[:, i, 0:1], ga[:, i, 3 * GH:GW], dif[:, t:t + 1], fn[:, t:t + 1],
                                                            ALU.mult, ALU.add), a, rw)
                        c = Q.dve(lambda e: e.reciprocal(dn[:, i, 1:2], dn[:, i, 0:1]), c)
                        d = Q.dve(lambda e: e.tensor_scalar(nb[:, i, :], G(1), dn[:, i, 1:2], None, ALU.mult), c, d, last.get(("nb", i)))
                        last[("ga", i)] = d
                        s["nb"] = d

                    def mean():
                        for i in range(2):
                            mean_of(i)

                    def project():
                        for i in range(2):
                            m = Q.pe(lambda e, i=i: e.transpose(ps_t[0:GH, i * P:(i + 1) * P], nb[:, i, :], identf[:]), s["nb"],
                                     last.get("ps_t"), end=i == 1)
                        last[("nb", 0)] = last[("nb", 1)] = m
                        a = Q.act(lambda e: e.activation(nbT[:], ps_t[0:GH, 0:2 * P], ACT.Copy), m, last.get("nbT"))
                        last["ps_t"] = a
                        p = Q.pool(lambda e: e.tensor_tensor(xbp[:], xp, row(0), ALU.add), last.get("xbp"))
                        for i in range(2):
                            m = Q.pe(lambda e, i=i: e.matmul(ps_o[:, 0, i * D:(i + 1) * D], nbT[:, i * P:(i + 1) * P], g_wp[:],
                                                             start=True, stop=True), a, last.get("ps_o0"), end=i == 1)
                        last["nbT"] = m
                        d = Q.dve(lambda e: e.tensor_tensor(xp, ps_o[:, 0, :].rearrange("p (i n) -> p i n", i=2), xbp[:], ALU.add), m, p)
                        last["ps_o0"] = last["xbp"] = d
                        n = normalise(xp, d)
                        p = Q.pool(lambda e: e.tensor_tensor(xp, xn[:], row(1), ALU.mult), n)
                        last["xn"] = p
                        s["y"] = Q.pool(lambda e: e.tensor_tensor(xp, xp, row(2), ALU.add), p)

                    return [mean, project] + qkv_stages(g, next_table, lambda: s["y"], qw)

                for g in range(PAIRS):
                    sums = [aggregate(2 * g), aggregate(2 * g + 1)]
                    for f in rest(g, sums):
                        f()
                finish(Q, nc, [s_w2] + s_at + s_kv)
            last.clear()

        transformer_layer(0, 0, None)
        gat_layer(1)
        transformer_layer(1, 1, 0)
        transformer_layer(2, 0, None)


def finish(Q, nc, dma_counters):
    for c in dma_counters:
        if c.value:
            Q.put("sync", [(c, c.value)], lambda e: e.nop())
    with nc.Block() as block:
        Q.emit(block)


def kernel(**inputs):
    import concourse.bacc as bacc
    from concourse.bass_utils import run_bass_kernel_spmd as run

    nc = bacc.Bacc("TRN2", target_bir_lowering=False, num_devices=1)
    arrays = {}

    def put(name, a):
        a = np.ascontiguousarray(a)
        arrays[name] = a
        return nc.dram_tensor(name, a.shape, mybir.dt.from_np(a.dtype), kind="ExternalInput").ap()

    x, adj = np.asarray(inputs["x"]), np.asarray(inputs["adj"])
    n, d = x.shape
    padded = -(-n // P) * P
    xp = np.zeros((padded, d), x.dtype)
    xp[:n] = x
    ap = np.eye(padded, dtype=adj.dtype)
    ap[:n, :n] = adj
    x_d, adj_d = put("x_in", xp), put("adj_in", ap)

    def columns(v):
        return np.asarray(v).reshape(-1, P).T

    def rows(v):
        return np.broadcast_to(np.asarray(v).reshape(1, -1), (P, np.asarray(v).size))

    layers = []
    for L in ("L0", "L2", "L3"):
        a = {k: np.asarray(inputs[f"{L}_gnn_{k}"]) for k in
             ("w_qkv", "w_proj", "b_proj", "w1", "b1", "w2", "b2", "g1", "be1", "g2", "be2")}
        cols = np.concatenate([columns(a[k]) for k in ("b1", "g2", "be2", "g1", "be1")], axis=1)
        rws = np.stack([rows(a["b_proj"]), rows(a["b2"])], axis=1)
        layers.append({**{k: put(f"{L}_{k}", a[k]) for k in ("w_qkv", "w_proj", "w1", "w2")},
                       "cols": put(f"{L}_cols", cols), "rows": put(f"{L}_rows", rws)})
    g = {k: np.asarray(inputs[f"L1_gnn_{k}"]) for k in ("Wt", "bt", "Wa", "ba", "Wp", "bp", "gamma", "beta")}
    gat = {"wt": put("L1_wt", g["Wt"].T), "wp": put("L1_wp", g["Wp"].T),
           "rows": put("L1_rows", np.concatenate([rows(g[k]) for k in ("bt", "Wa", "ba", "bp", "gamma", "beta")], axis=1))}
    out_d = nc.dram_tensor("out", (n, d), F32, kind="ExternalOutput").ap()
    graph_layers(nc, x_d, adj_d, layers, gat, out_d, n)
    return run(nc, [arrays], core_ids=[0]).results[0]["out"]
```

```python
from contextlib import ExitStack

import numpy as np

import concourse.bass as bass
from concourse import mybir

ALU = mybir.AluOpType
ACT = mybir.ActivationFunctionType
F32 = mybir.dt.float32
BF16 = mybir.dt.bfloat16
F8 = mybir.dt.float8e4
I32 = mybir.dt.int32
U32 = mybir.dt.uint32
AX_X = mybir.AxisListType.X
RMAX = bass.bass_isa.ReduceOp.max

P = 128
HEADS = 8
GROUP = 4
EPS = 1e-5
NEG = -9e15
MASKED = -1e30
RSQRT_MAGIC = float(0x5F3759DF)
GELU_CUBE = 0.044715
GELU_SCALE = 0.7978845608028654
SEGMENT = 256
NEIGHBOURS = 24
EDGE_TILES = 10
RING = 16
AHEAD = 5
SCORE_LIMIT = 60.0


class Counter:

    def __init__(self, sem):
        self.sem, self.value = sem, 0

    def up(self, by):
        self.value += by
        return (self, self.value)


class Queues:

    def __init__(self, ends):
        self.ends = ends
        self.steps = {k: [] for k in ("sync", "pe", "dve", "act", "pool")}

    def put(self, engine, waits, make, counter=None, by=1):
        mark = counter.up(by) if counter is not None else None
        self.steps[engine].append(([w for w in waits if w is not None], make, counter, by))
        return mark

    def pe(self, make, *waits, end=True):
        return self.put("pe", waits, make, self.ends["pe"] if end else None)

    def dve(self, make, *waits):
        return self.put("dve", waits, make, self.ends["dve"])

    def act(self, make, *waits):
        return self.put("act", waits, make, self.ends["act"])

    def pool(self, make, *waits):
        return self.put("pool", waits, make, self.ends["pool"])

    def load(self, out, in_, landed, *waits, engine="sync"):
        return self.put(engine, waits, lambda e: e.dma_start(out, in_), landed, 16)

    def emit(self, block):
        for name, on in (("sync", block.sync), ("pe", block.tensor), ("dve", block.vector),
                         ("act", block.scalar), ("pool", block.gpsimd)):
            def program(e, steps=self.steps[name]):
                passed = {}
                for waits, make, counter, by in steps:
                    for c, value in waits:
                        if passed.get(id(c), 0) < value:
                            e.wait_ge(c.sem, value)
                            passed[id(c)] = value
                    ins = make(e)
                    if counter is not None:
                        ins.then_inc(counter.sem, by)
            on(program)
            self.steps[name] = []


def graph_layers(nc, x_d, adj_d, layers_d, gat_d, out_d, n_real):
    NP, D = x_d.shape
    T = NP // P
    PAIRS = T // 2
    HD = D // HEADS
    KD = D // P
    FF = layers_d[0]["w1"].shape[1]
    KF = FF // P
    GH = gat_d["wt"].shape[1]
    SCALE = float(HD) ** -0.5
    GW = 3 * GH + 1

    kv_d = [nc.dram_tensor(f"kv_rows_{i}", [NP, 2 * D], F32).ap() for i in range(2)]
    adjT_d = nc.dram_tensor("adj_transposed", [T, P, NP], F8).ap()
    EDGES = EDGE_TILES * P
    SEGS = NP // SEGMENT
    DUOS = EDGE_TILES // 2
    ROW = 2 * D + HEADS
    att_d = nc.dram_tensor("dense_attention_out", [NP, D], F32).ap()

    with ExitStack() as top:
        def sem(n):
            return top.enter_context(nc.semaphore(n))

        times = {}

        def sbuf(n, shape, dt=F32, where=top):
            times[n] = times.get(n, 0) + 1
            n += f"_{times[n]}" if times[n] > 1 else ""
            return where.enter_context(nc.sbuf_tensor(n, shape, dt))

        x = sbuf("x_nodes", [P, T, D])
        q_all = sbuf("queries", [P, T, D])
        sel = sbuf("node_to_edge", [P, T, EDGES], F8)
        src_row = sbuf("edge_source_row", [P, T * EDGE_TILES], I32)
        dst_no = sbuf("edge_target_number", [P, T * EDGE_TILES])
        over = sbuf("edge_list_overflow", [P, 2, T])
        norms = sbuf("squared_norms", [P, T, 2 * HEADS])
        iota_n = sbuf("node_numbers", [P, P])
        flag = sbuf("dense_needed", [P, 2 * HEADS + 4])
        flag_u = sbuf("dense_needed_int", [P, 1], U32)
        identf = sbuf("identity_f32", [P, P])
        identb = sbuf("identity_bf16", [P, P], BF16)
        w_qkv = sbuf("w_qkv", [P, KD, 3 * D])
        w_proj = sbuf("w_proj", [P, KD, D])
        w_1 = sbuf("w_1", [P, KD, FF])
        w_2 = sbuf("w_2", [P, KF, D])
        cols = sbuf("bias_and_norm_columns", [P, KF + 4 * KD])
        rows = sbuf("bias_rows", [P, 2, D])
        att = sbuf("attention_pair", [P, 2, 2, D])
        attT = sbuf("attention_transposed", [P, KD, 2 * P])
        xn = sbuf("normalised", [P, 2, D])
        h2T = sbuf("ff_input_transposed", [P, KD, 2 * P])
        h1T = sbuf("qkv_input_transposed", [P, KD, 2 * P])
        ffh = sbuf("ff_hidden", [P, KF, 2 * P])
        ffu = sbuf("ff_gelu_argument", [P, KF // 2, 2 * P])
        xb = sbuf("x_plus_bias", [P, 2, D])
        kv_st = sbuf("kv_to_store", [P, 2, 2 * D])
        sq = sbuf("qk_squares", [P, 2 * D])
        q_rest = sbuf("query_rest", [P, D])
        stat = sbuf("norm_statistics", [P, 2, 6])
        mv = sbuf("mean_and_variance", [P, 2, 2])
        nw = sbuf("rsqrt_work", [P, 6, 2])
        gh = sbuf("h_parts_and_one", [P, T, GW], BF16)
        gs = sbuf("gat_row_scores", [P, T])

        psum = lambda n, shape: top.enter_context(nc.psum_tensor(n, shape, F32))
        ps_q = psum("ps_q", [P, 2, 512])
        ps_a = psum("ps_a", [P, 512])
        ps_t = psum("ps_t", [P, 512])
        ps_w = psum("ps_w", [P, 2, 512])
        ps_o = psum("ps_o", [P, 2, 512])

        ends = {k: Counter(sem("steps_done_" + k)) for k in ("pe", "dve", "act", "pool")}
        loop_ends = {k: sem("dense_steps_done_" + k) for k in ("pe", "dve", "act", "pool")}
        loop_dma = [sem(f"dense_loaded_{i}") for i in range(3)]
        loop_sems = range(loop_ends["pe"].num, loop_dma[-1].num + 1)
        s_w = Counter(sem("weights_landed"))
        s_w2 = Counter(sem("qkv_weights_landed"))
        s_x = Counter(sem("x_landed"))
        s_adj = [Counter(sem(f"adj_landed_{i}")) for i in range(2)]
        s_at = [Counter(sem(f"adj_transposed_moved_{i}")) for i in range(3)]
        s_kv = [Counter(sem(f"kv_stored_{i}")) for i in range(2)]
        s_dense = Counter(sem("dense_attention_landed"))
        s_ring = [Counter(sem(f"edges_landed_{i}")) for i in range(RING)]
        s_out = Counter(sem("out_stored"))
        Q = Queues(ends)
        last = {}

        cb1, cg2, cbe2, cg1, cbe1 = 0, KF, KF + KD, KF + 2 * KD, KF + 3 * KD

        def load_main_weights(L):
            d = layers_d[L]
            Q.load(w_proj[:], d["w_proj"].rearrange("(k p) n -> p k n", p=P), s_w)
            Q.load(cols[:, 0:cg1], d["cols"][:, 0:cg1], s_w)
            Q.load(rows[:], d["rows"], s_w)
            Q.load(w_1[:], d["w1"].rearrange("(k p) n -> p k n", p=P), s_w)
            return Q.load(w_2[:], d["w2"].rearrange("(k p) n -> p k n", p=P), s_w)

        def load_qkv_weights(L):
            d = layers_d[L]
            Q.load(cols[:, cg1:], d["cols"][:, cg1:], s_w2)
            return Q.load(w_qkv[:], d["w_qkv"].rearrange("(k p) n -> p k n", p=P), s_w2)

        def normalise(src, ready):
            m = ready
            for i in range(2):
                m = Q.dve(lambda e, i=i: e.bn_stats(stat[:, i, :], src[:, i, :]), ready)
            for i in range(2):
                m = Q.dve(lambda e, i=i: e.bn_aggr(mv[:, i, :], stat[:, i, :]), m)
            var = mv[:, :, 1]
            v, hv, y, a, sh = (nw[:, j, :] for j in range(5))
            Q.dve(lambda e: e.tensor_scalar(v, var, EPS, None, ALU.add), m)
            m = Q.dve(lambda e: e.tensor_scalar(hv, var, EPS, -0.5, ALU.add, ALU.mult), m)
            m = Q.dve(lambda e: e.tensor_scalar(sh.bitcast(I32), v.bitcast(I32), 1, None, ALU.logical_shift_right), m)
            m = Q.dve(lambda e: e.tensor_scalar(y.bitcast(I32), sh.bitcast(I32), -1.0, RSQRT_MAGIC, ALU.mult, ALU.add), m)
            for _ in range(3):
                m = Q.dve(lambda e: e.tensor_tensor(a, y, y, ALU.mult), m)
                m = Q.dve(lambda e: e.tensor_tensor(a, a, hv, ALU.mult), m)
                m = Q.dve(lambda e: e.scalar_tensor_tensor(out=y, in0=a, scalar=1.5, in1=y, op0=ALU.add, op1=ALU.mult), m)
            for i in range(2):
                w = Q.dve(lambda e, i=i: e.tensor_scalar(xn[:, i, :], src[:, i, :], mv[:, i, 0:1], y[:, i:i + 1],
                                                         ALU.subtract, ALU.mult), m, last.get("xn"))
            return w

        def transpose_pair(src, ready, width=D):
            for k in range(KD):
                for i in range(2):
                    o = (2 * k + i) * P
                    m = Q.pe(lambda e, k=k, i=i, o=o: e.transpose(ps_t[:, o:o + P], src[:, i, k * P:(k + 1) * P], identf[:]),
                             ready, last.get("ps_t"), end=(k, i) == (KD - 1, 1))
            return m

        def scaled_out(dst, name, g_col, b_col, turned, ready):
            for k in range(KD):
                m = Q.act(lambda e, k=k: e.activation(dst[:, k, :], ps_t[:, k * 2 * P:(k + 1) * 2 * P], ACT.Identity,
                                                      bias=cols[:, b_col + k:b_col + k + 1],
                                                      scale=cols[:, g_col + k:g_col + k + 1]),
                          turned, last.get(name), ready)
            last["ps_t"] = m
            return m

        def qkv_stages(g, table, after, qkv_w):
            s = {}

            def norm():
                s["n"] = normalise(x[:, 2 * g:2 * g + 2, :], after())

            def turn():
                t = transpose_pair(xn, s["n"])
                last["xn"] = t
                s["h"] = scaled_out(h1T, "h1T", cg1, cbe1, t, qkv_w)

            def tile(i):
                t = 2 * g + i
                for c0, c1 in ((0, 512), (512, 768)):
                    for k in range(KD):
                        m = Q.pe(lambda e, i=i, k=k, c0=c0, c1=c1: e.matmul(
                            ps_o[:, c0 // 512, 0:c1 - c0], h1T[:, k, i * P:(i + 1) * P], w_qkv[:, k, c0:c1],
                            start=(k == 0), stop=(k == KD - 1)), s["h"], qkv_w, last.get("ps_o0"), last.get("ps_o1"),
                            end=(c0 and k == KD - 1))
                last["h1T"] = m
                Q.act(lambda e: e.activation(q_all[:, t, :], ps_o[:, 0, 0:D], ACT.Copy), m, last.get(("q", t)))
                a1 = Q.act(lambda e: e.activation(sq[:], ps_o[:, 0, :], ACT.Square), m, last.get("sq"))
                a2 = Q.act(lambda e: e.activation(kv_st[:, i, 0:D], ps_o[:, 0, D:2 * D], ACT.Copy), m, last.get(("kv_st", i)))
                a3 = Q.act(lambda e: e.activation(kv_st[:, i, D:2 * D], ps_o[:, 1, 0:D], ACT.Copy), m)
                last["sq"] = last["norms"] = Q.dve(lambda e: e.tensor_reduce(norms[:, t, :], sq[:].rearrange("p (h c) -> p h c", c=HD),
                                                                             AX_X, ALU.add), a1)
                last["ps_o0"], last["ps_o1"] = a2, a3
                last[("kv_st", i)] = Q.load(kv_d[table][t * P:(t + 1) * P, :], kv_st[:, i, :], s_kv[i], a2, a3)

            return [norm, turn, lambda: tile(0), lambda: tile(1)]

        def gat_input_stages(g, after, gw):
            s = {}

            def turn():
                t = transpose_pair(x[:, 2 * g:2 * g + 2, :], after())
                s["h"] = Q.act(lambda e: e.activation(h1T[:].rearrange("p k n -> p (k n)"), ps_t[:], ACT.Copy), t, last.get("h1T"))
                last["ps_t"] = s["h"]

            def tile(i):
                t = 2 * g + i
                for k in range(KD):
                    m = Q.pe(lambda e, k=k: e.matmul(ps_o[:, 0, 0:GH], h1T[:, k, i * P:(i + 1) * P], g_wt[:, k, :],
                                                     start=(k == 0), stop=(k == KD - 1)), s["h"], gw, last.get("ps_o0"),
                             end=k == KD - 1)
                last["h1T"] = m
                hf = g_work[:, i, 0:GH]
                hr = g_work[:, i, GH:2 * GH]
                hw = g_work[:, i, 2 * GH:3 * GH]
                d = Q.dve(lambda e: e.tensor_tensor(hf, ps_o[:, 0, 0:GH], g_rows[:, 0:GH], ALU.add), m, gw, last.get(("gw", i)))
                last["ps_o0"] = d
                a = Q.dve(lambda e: e.tensor_tensor_reduce(hw, hf, g_rows[:, GH:2 * GH], 1.0, 0.0, ALU.mult, ALU.add,
                                                           gs[:, t:t + 1]), d)
                p = Q.pool(lambda e: e.tensor_copy(gh[:, t, 0:GH], hf), d)
                p = Q.pool(lambda e: e.tensor_tensor(hr, hf, gh[:, t, 0:GH], ALU.subtract), p, d)
                p = Q.pool(lambda e: e.tensor_copy(gh[:, t, GH:2 * GH], hr), p)
                p = Q.pool(lambda e: e.tensor_tensor(gh[:, t, 2 * GH:3 * GH], hr, gh[:, t, GH:2 * GH], ALU.subtract), p)
                last[("gw", i)] = p
                last["gs"] = a
                last["gh"] = p

            return [turn, lambda: tile(0), lambda: tile(1)]

        def mlp_stages(g, att_ready, wts, then):
            s = {}
            b = g % 2
            xp = x[:, 2 * g:2 * g + 2, :]
            row = lambda j: rows[:, j, :].unsqueeze(1).to_broadcast([P, 2, D])

            def project():
                t = transpose_pair(att[:, b], att_ready())
                last[("att", b)] = t
                a = Q.act(lambda e: e.activation(attT[:].rearrange("p k n -> p (k n)"), ps_t[:], ACT.Copy), t, last.get("attT"))
                last["ps_t"] = a
                p = Q.pool(lambda e: e.tensor_tensor(xb[:], xp, row(0), ALU.add), wts, last.get("xb"))
                for i in range(2):
                    for k in range(KD):
                        m = Q.pe(lambda e, i=i, k=k: e.matmul(ps_o[:, 0, i * D:(i + 1) * D], attT[:, k, i * P:(i + 1) * P],
                                                              w_proj[:, k, :], start=(k == 0), stop=(k == KD - 1)),
                                 a, wts, last.get("ps_o0"), end=(i == 1 and k == KD - 1))
                last["attT"] = m
                d = Q.dve(lambda e: e.tensor_tensor(xp, ps_o[:, 0, :].rearrange("p (i n) -> p i n", i=2), xb[:], ALU.add), m, p)
                last["ps_o0"] = d
                s["x1"] = d
                s["xb2"] = Q.pool(lambda e: e.tensor_tensor(xb[:], xp, row(1), ALU.add), d)

            def norm():
                s["n"] = normalise(xp, s["x1"])

            def turn():
                t = transpose_pair(xn, s["n"])
                last["xn"] = t
                s["h"] = scaled_out(h2T, "h2T", cg2, cbe2, t, wts)

            def up(c):
                bank = c % 2
                for j in range(2):
                    f = 2 * c + j
                    for k in range(KD):
                        m = Q.pe(lambda e, j=j, f=f, k=k: e.matmul(ps_w[:, bank, j * 2 * P:(j + 1) * 2 * P],
                                                                   w_1[:, k, f * P:(f + 1) * P], h2T[:, k, :],
                                                                   start=(k == 0), stop=(k == KD - 1)),
                                 s["h"], wts, last.get(("ps_w", bank)), end=(j == 1 and k == KD - 1))
                last["h2T"] = m
                for j in range(2):
                    f = 2 * c + j
                    src = ps_w[:, bank, j * 2 * P:(j + 1) * 2 * P]
                    Q.act(lambda e, f=f, src=src: e.activation(ffh[:, f, :], src, ACT.Identity, bias=cols[:, cb1 + f:cb1 + f + 1]),
                          m, last.get(("ffh", f // 4)))
                    a = Q.act(lambda e, f=f, src=src: e.activation(ffu[:, f % 4, :], src, ACT.Square, bias=cols[:, cb1 + f:cb1 + f + 1]),
                              m, last.get("ffu"))
                last[("ps_w", bank)] = a
                if c % 2:
                    half = c // 2
                    hh, uu = ffh[:, 4 * half:4 * half + 4, :], ffu[:]
                    p = Q.dve(lambda e: e.scalar_tensor_tensor(out=uu, in0=uu, scalar=1.0 / GELU_CUBE, in1=hh, op0=ALU.add,
                                                                op1=ALU.mult), a)
                    a = Q.act(lambda e: e.activation(uu, uu, ACT.Tanh, scale=GELU_SCALE * GELU_CUBE), p)
                    s[("g", half)] = Q.dve(lambda e: e.scalar_tensor_tensor(out=hh, in0=uu, scalar=1.0, in1=hh, op0=ALU.add,
                                                                            op1=ALU.mult), a)
                    last["ffu"] = s[("g", half)]

            def down():
                for i in range(2):
                    for f in range(KF):
                        m = Q.pe(lambda e, i=i, f=f: e.matmul(ps_o[:, 1, i * D:(i + 1) * D], ffh[:, f, i * P:(i + 1) * P],
                                                              w_2[:, f, :], start=(f == 0), stop=(f == KF - 1)),
                                 s[("g", f // 4)], wts, last.get("ps_o1"), end=(i == 1 and f == KF - 1))
                last[("ffh", 0)] = last[("ffh", 1)] = m
                d = Q.dve(lambda e: e.scalar_tensor_tensor(out=xp, in0=ps_o[:, 1, :].rearrange("p (i n) -> p i n", i=2),
                                                           scalar=0.5, in1=xb[:], op0=ALU.mult, op1=ALU.add), m, s["xb2"])
                last["ps_o1"] = last["xb"] = d
                s["x2"] = d

            return [project, norm, turn, lambda: up(0), lambda: up(1), lambda: up(2), lambda: up(3), down] + then(lambda: s["x2"])

        def dense_test(list_overflow=False):
            H2 = 2 * HEADS
            m = last["norms"]
            if list_overflow:
                m = Q.dve(lambda e: e.tensor_reduce(flag[:, H2 + 3:H2 + 4], over[:].rearrange("p a t -> p (a t)"), AX_X, ALU.max), last["over"])
                m = Q.pool(lambda e: e.partition_all_reduce(flag[:, H2 + 2:H2 + 3], flag[:, H2 + 3:H2 + 4], P, RMAX), m)
            m = Q.dve(lambda e: e.tensor_reduce(sq[:, 0:H2], norms[:].rearrange("p t c -> p c t"), AX_X, ALU.max), last["norms"], m)
            m = Q.pool(lambda e: e.partition_all_reduce(flag[:, 0:H2], sq[:, 0:H2], P, RMAX), m)
            m = Q.dve(lambda e: e.tensor_tensor(flag[:, 0:HEADS], flag[:, 0:HEADS], flag[:, HEADS:H2], ALU.mult), m)
            m = Q.dve(lambda e: e.tensor_reduce(flag[:, H2:H2 + 1], flag[:, 0:HEADS], AX_X, ALU.max), m)
            m = Q.dve(lambda e: e.tensor_scalar(flag[:, H2 + 1:H2 + 2], flag[:, H2:H2 + 1], (SCORE_LIMIT / SCALE) ** 2, None, ALU.is_gt), m)
            Q.dve(lambda e: e.tensor_tensor(flag_u[:], flag[:, H2 + 1:H2 + 2], flag[:, H2 + 2:H2 + 3], ALU.max), m)

        def store_stage(g, after):
            def store():
                for i in range(2):
                    t = 2 * g + i
                    n = min(P, n_real - t * P)
                    last["out"] = Q.load(out_d[t * P:t * P + n, :], x[0:n, t, :], s_out, after())
            return [store]

        with ExitStack() as ph:
            adj_i = sbuf("adj_rows", [P, 2, NP], I32, ph)
            adj_b = sbuf("adj_rows_bf16", [P, NP], BF16, ph)
            at_st = sbuf("adj_transposed_tile", [P, NP], F8, ph)
            found = gh[:].rearrange("p t c -> p (t c)")[:, 0:NP]
            iota_e = ffh[:].rearrange("p f n -> p (f n)")[:, 0:EDGES]
            begun = ffu[:].rearrange("p f n -> p (f n)").bitcast(BF16)[:, 0:EDGES]
            iota_s = sbuf("column_in_segment", [P, SEGMENT], BF16, ph)
            seg_base = sbuf("segment_base", [P, SEGS, 8], F32, ph)
            iota_j = sbuf("neighbour_numbers", [P, NEIGHBOURS], F32, ph)
            slot = sbuf("slot_numbers", [P, EDGE_TILES], F32, ph)
            earlier = sbuf("earlier_nodes", [P, P], BF16, ph)
            one = sbuf("one_column", [P, 1], BF16, ph)
            cand = sbuf("edge_candidates", [P, 3, SEGS * 8], F32, ph)
            nbr = sbuf("neighbour_list", [P, NEIGHBOURS + 2], F32, ph)
            parts = sbuf("neighbour_list_parts", [P, 2, NEIGHBOURS + 2], BF16, ph)
            cnt_w = sbuf("edge_counts", [P, 6 + NEIGHBOURS], F32, ph)
            cnt_b = sbuf("edge_counts_bf16", [P, 1], BF16, ph)
            pick = sbuf("picked_neighbour", [P, EDGE_TILES, NEIGHBOURS], F32, ph)
            offs = sbuf("edge_offsets", [P, 3, EDGE_TILES], F32, ph)
            NB = NEIGHBOURS

            def iota(dst, pattern, base, per_partition=0):
                return Q.pool(lambda e: e.iota(dst, pattern, base=base, channel_multiplier=per_partition,
                                               allow_small_or_imprecise_dtypes=True))

            p1 = Q.pool(lambda e: e.memset(identf[:], 0.0))
            p1 = Q.pool(lambda e: e.affine_select(out=identf[:], in_=identf[:], compare_op=ALU.not_equal, fill=1.0, base=0,
                                                  pattern=[[-1, P]], channel_multiplier=1), p1)
            Q.pool(lambda e: e.tensor_copy(identb[:], identf[:]), p1)
            p1 = Q.pool(lambda e: e.memset(earlier[:], 1.0))
            Q.pool(lambda e: e.affine_select(out=earlier[:], in_=earlier[:], compare_op=ALU.is_gt, fill=0.0, base=0,
                                             pattern=[[1, P]], channel_multiplier=-1), p1)
            Q.pool(lambda e: e.memset(one[:], 1.0))
            Q.pool(lambda e: e.memset(parts[:], 0.0))
            iota(iota_s[:], [[1, SEGMENT]], 1)
            iota(seg_base[:], [[SEGMENT, SEGS], [0, 8]], 0)
            iota(iota_j[:], [[1, NB]], 0)
            iota(slot[:], [[P, EDGE_TILES]], 0, 1)
            iota(iota_e, [[1, EDGES]], 0)
            iota(iota_n[:], [[1, P]], 1)
            consts = iota(nbr[:, NB + 1:NB + 2], [[0, 1]], 1, 1)
            for g in range(PAIRS):
                xl = Q.load(x[:, 2 * g:2 * g + 2, :], x_d[2 * g * P:(2 * g + 2) * P, :].rearrange("(i p) d -> p i d", p=P), s_x,
                            engine="act")
                if g == 0:
                    qw = load_qkv_weights(0)
                    load_main_weights(0)
            xl_all = xl

            def adjacency(t):
                b = t % 2
                landed = Q.load(adj_i[:, b, :], adj_d[t * P:(t + 1) * P, :], s_adj[b], last.get(("adj_i", b)))
                a = Q.act(lambda e: e.activation(adj_b[:], adj_i[:, b, :], ACT.Sign), landed, last.get("adj_b_pe"), last.get("adj_b_pool"))
                last[("adj_i", b)] = a
                f = Q.pool(lambda e: e.tensor_tensor(found.rearrange("p (s c) -> p s c", c=SEGMENT),
                                                     adj_b[:].rearrange("p (s c) -> p s c", c=SEGMENT),
                                                     iota_s[:].unsqueeze(1).to_broadcast([P, SEGS, SEGMENT]), ALU.mult),
                           a, consts, last.get("found"))
                last["adj_b_pool"] = f
                for n, m0 in enumerate(range(0, T, 8)):
                    bank = n % 2
                    view = ps_w[:, bank, :].bitcast(BF16)
                    cnt = min(8, T - m0)
                    for m in range(cnt):
                        tr = Q.pe(lambda e, m=m, m0=m0, view=view: e.transpose(
                            view[:, m * P:(m + 1) * P], adj_b[:, (m0 + m) * P:(m0 + m + 1) * P], identb[:]),
                            a, consts, last.get(("ps_w", bank)), end=m == cnt - 1)
                    dst = at_st[:, m0 * P:(m0 + cnt) * P]
                    last[("ps_w", bank)] = Q.act(lambda e, dst=dst, view=view, cnt=cnt: e.activation(
                        dst, view[:, 0:cnt * P], ACT.Copy, saturate=False), tr, last.get("at_st"), last.get("at_st_pe"))
                last["adj_b_pe"] = tr
                last["at_st"] = Q.load(adjT_d[t], at_st[:], s_at[0], last[("ps_w", 0)], last[("ps_w", 1)])
                for m in range(T):
                    c = Q.pe(lambda e, m=m: e.matmul(ps_a[:, 1:2], at_st[:, m * P:(m + 1) * P], one[:], start=(m == 0), stop=(m == T - 1)),
                             last[("ps_w", 0)], last[("ps_w", 1)], last.get("ps_a"), end=m == T - 1)
                last["at_st_pe"] = c
                return f, c

            def edge_list(t, f, true_count):
                for k in range(SEGS):
                    d = Q.dve(lambda e, k=k: e.max(cand[:, 0, 8 * k:8 * k + 8], found[:, k * SEGMENT:(k + 1) * SEGMENT]), f)
                last["found"] = d
                flat = seg_base[:].rearrange("p s c -> p (s c)")
                d = Q.dve(lambda e: e.scalar_tensor_tensor(out=cand[:, 1, :], in0=cand[:, 0, :], scalar=0.0, in1=flat,
                                                           op0=ALU.is_gt, op1=ALU.mult), d)
                d = Q.dve(lambda e: e.tensor_tensor(cand[:, 0, :], cand[:, 0, :], cand[:, 1, :], ALU.add), d)
                for r in range(NB // 8):
                    a, b = (0, 1) if r % 2 == 0 else (1, 0)
                    d = Q.dve(lambda e, a=a, r=r: e.max(nbr[:, 8 * r:8 * r + 8], cand[:, a, :]), d)
                    if r < NB // 8 - 1:
                        d = Q.dve(lambda e, a=a, b=b, r=r: e.match_replace(out=cand[:, b, :], in_to_replace=nbr[:, 8 * r:8 * r + 8],
                                                                           in_values=cand[:, a, :], imm_value=0.0), d)
                d = Q.dve(lambda e: e.tensor_scalar(cnt_w[:, 6:], nbr[:, 0:NB], 0.0, None, ALU.is_gt), d)
                cnt = Q.dve(lambda e: e.tensor_reduce(cnt_w[:, 0:1], cnt_w[:, 6:], AX_X, ALU.add), d)
                cb = Q.dve(lambda e: e.tensor_copy(cnt_b[:], cnt_w[:, 0:1]), cnt)
                m = Q.pe(lambda e: e.matmul(ps_a[:, 0:1], earlier[:], cnt_b[:], start=True, stop=True), cb, true_count)
                st = Q.dve(lambda e: e.tensor_copy(nbr[:, NB:NB + 1], ps_a[:, 0:1]), m)
                tc = Q.dve(lambda e: e.tensor_copy(cnt_w[:, 1:2], ps_a[:, 1:2]), m)
                last["ps_a"] = tc
                en = Q.dve(lambda e: e.tensor_tensor(cnt_w[:, 2:3], nbr[:, NB:NB + 1], cnt_w[:, 0:1], ALU.add), st)
                Q.dve(lambda e: e.tensor_tensor(over[:, 0, t:t + 1], cnt_w[:, 1:2], cnt_w[:, 0:1], ALU.not_equal), tc)
                last["over"] = Q.dve(lambda e: e.tensor_scalar(over[:, 1, t:t + 1], cnt_w[:, 2:3], float(EDGES), None, ALU.is_gt), en)
                d = Q.dve(lambda e: e.tensor_copy(parts[:, 0, :], nbr[:]), en, last.get("parts"))
                pr = Q.dve(lambda e: e.tensor_tensor(parts[:, 1, :], nbr[:], parts[:, 0, :], ALU.subtract), d)
                d = Q.dve(lambda e: e.tensor_scalar(begun, iota_e, nbr[:, NB:NB + 1], None, ALU.is_ge), en)
                sl = Q.dve(lambda e: e.scalar_tensor_tensor(out=sel[:, t, :], in0=iota_e, scalar=cnt_w[:, 2:3], in1=begun,
                                                            op0=ALU.is_lt, op1=ALU.mult, saturate=False), d)
                W = NB + 2
                for k in range(EDGE_TILES):
                    for j in range(2):
                        m = Q.pe(lambda e, k=k, j=j: e.matmul(ps_q[:, 0, k * W:(k + 1) * W], sel[:, t, k * P:(k + 1) * P], parts[:, j, :],
                                                              start=(j == 0), stop=(j == 1)), sl, pr, last.get("ps_q0"),
                                 end=(k == EDGE_TILES - 1 and j == 1))
                last["parts"] = m
                G = ps_q[:, 0, 0:EDGE_TILES * W].rearrange("p (k c) -> p k c", c=W)
                d = Q.dve(lambda e: e.tensor_tensor(offs[:, 0, :], slot[:], G[:, :, NB], ALU.subtract), m)
                d = Q.dve(lambda e: e.tensor_tensor(pick[:], iota_j[:].unsqueeze(1).to_broadcast([P, EDGE_TILES, NB]),
                                                    offs[:, 0, :].unsqueeze(2).to_broadcast([P, EDGE_TILES, NB]), ALU.is_equal), d)
                d = Q.dve(lambda e: e.tensor_tensor(pick[:], pick[:], G[:, :, 0:NB], ALU.mult), d)
                d2 = Q.dve(lambda e: e.tensor_copy(dst_no[:, t * EDGE_TILES:(t + 1) * EDGE_TILES], G[:, :, NB + 1]), m)
                last["ps_q0"] = d2
                d = Q.dve(lambda e: e.tensor_reduce(offs[:, 1, :], pick[:], AX_X, ALU.add), d)
                Q.dve(lambda e: e.tensor_scalar(src_row[:, t * EDGE_TILES:(t + 1) * EDGE_TILES], offs[:, 1, :], -1.0, 0.0,
                                                ALU.add, ALU.max), d)

            for g in range(PAIRS):
                st = qkv_stages(g, 0, lambda: xl_all, qw)
                fc = adjacency(2 * g)
                st[0](); st[1]()
                edge_list(2 * g, *fc)
                fc = adjacency(2 * g + 1)
                st[2](); st[3]()
                edge_list(2 * g + 1, *fc)
            p = last["found"]
            Q.pool(lambda e: e.memset(gh[:], 1.0), p)
            dense_test(list_overflow=True)
            finish(Q, nc, [s_x, s_w, s_w2] + s_adj + s_at + s_kv)
        last.clear()

        def dense_attention(table):
            S0, S1, S2 = (lambda: Counter(loop_dma[0])), (lambda: Counter(loop_dma[1])), (lambda: Counter(loop_dma[2]))
            with ExitStack() as ph:
                mask = sbuf("dense_mask", [P, NP], I32, ph)
                kT = sbuf("dense_keys_transposed", [P, NP], F32, ph)
                vg = sbuf("dense_values", [P, T, P], F32, ph)
                st = sbuf("dense_row_statistics", [P, 4], F32, ph)
                qp = sbuf("dense_q_tile", [P, P], F32, ph)
                qT = sbuf("dense_q_transposed", [P, P], F32, ph)
                og = sbuf("dense_out_tile", [P, P], F32, ph)
                pT = ffu[:].rearrange("p f n -> p (f n)").rearrange("p (b n) -> p b n", b=2)
                banks = [ps_q[:, 0, :], ps_q[:, 1, :], ps_a[:], ps_t[:], ps_w[:, 0, :], ps_w[:, 1, :], ps_o[:, 0, :]]
                sc = mask[:].bitcast(F32)
                for grp in range(HEADS // GROUP):
                    c0 = grp * P
                    q = Queues({k: Counter(s) for k, s in loop_ends.items()})
                    s0, s1, s2 = S0(), S1(), S2()
                    kl = q.load(sc.rearrange("p (t c) -> p t c", c=P),
                                kv_d[table][:, c0:c0 + P].rearrange("(t p) c -> p t c", p=P), s0)
                    vl = q.load(vg[:], kv_d[table][:, D + c0:D + c0 + P].rearrange("(t p) c -> p t c", p=P), s1)
                    evac = None
                    for m0 in range(0, T, 4):
                        cnt = min(4, T - m0)
                        for m in range(cnt):
                            tr = q.pe(lambda e, m=m, m0=m0: e.transpose(ps_t[:, m * P:(m + 1) * P], sc[:, (m0 + m) * P:(m0 + m + 1) * P],
                                                                        identf[:]), kl, evac, end=m == cnt - 1)
                        evac = q.dve(lambda e, m0=m0, cnt=cnt: e.tensor_copy(kT[:, m0 * P:(m0 + cnt) * P], ps_t[:, 0:cnt * P]), tr)
                    with nc.Block() as block:
                        q.put("sync", [vl, evac], lambda e: e.nop())
                        q.emit(block)
                    nc.all_engine_barrier(sems_to_clear=loop_sems)
                    with nc.Fori(0, T) as it:
                        q = Queues({k: Counter(s) for k, s in loop_ends.items()})
                        s0, s1, s2 = S0(), S1(), S2()
                        ql = q.load(qp[:], q_all[:, bass.ds(it, 1), c0:c0 + P], s1)
                        m = q.pe(lambda e: e.transpose(ps_o[:, 1, 0:P], qp[:], identf[:]), ql)
                        qt = q.dve(lambda e: e.tensor_copy(qT[:], ps_o[:, 1, 0:P]), m)
                        freed = ov = None
                        for h in range(GROUP):
                            r0 = h * HD
                            for c in range(0, NP, 512):
                                w = min(512, NP - c)
                                m = q.pe(lambda e, c=c, w=w, r0=r0: e.matmul(banks[c // 512][:, 0:w], qT[r0:r0 + HD, :], kT[r0:r0 + HD, c:c + w],
                                                                             start=True, stop=True), qt, freed, end=c + w == NP)
                            ml = q.load(mask[:], adj_d[bass.ds(it * P, P), :], s0, freed)
                            d = q.dve(lambda e: e.tensor_scalar(sc, mask[:], 0, MASKED, ALU.is_equal, ALU.mult), ml)
                            for c in range(0, NP, 512):
                                w = min(512, NP - c)
                                d = q.dve(lambda e, c=c, w=w: e.tensor_tensor_reduce(
                                    sc[:, c:c + w], banks[c // 512][:, 0:w], sc[:, c:c + w], 1.0,
                                    -3e38 if c == 0 else st[:, 0:1], ALU.add, ALU.max, st[:, 0:1]), m, d)
                            d = q.dve(lambda e: e.tensor_scalar(st[:, 1:2], st[:, 0:1], -SCALE, None, ALU.mult), d, freed)
                            a = q.act(lambda e: e.activation(sc, sc, ACT.Exp, bias=st[:, 1:2], scale=SCALE, accum_out=st[:, 2:3]), d)
                            rd = q.dve(lambda e: e.reciprocal(st[:, 3:4], st[:, 2:3]), a)
                            pv = [None, None]
                            for n, m0 in enumerate(range(0, T, 4)):
                                cnt = min(4, T - m0)
                                for m in range(cnt):
                                    tr = q.pe(lambda e, m=m, m0=m0, n=n: e.transpose(banks[n][:, m * P:(m + 1) * P],
                                                                                    sc[:, (m0 + m) * P:(m0 + m + 1) * P], identf[:]),
                                              a, d, end=m == cnt - 1)
                                ev = q.act(lambda e, n=n, cnt=cnt: e.activation(pT[:, n % 2, 0:cnt * P], banks[n][:, 0:cnt * P], ACT.Copy),
                                           tr, pv[n % 2])
                                for m in range(cnt):
                                    mm = q.pe(lambda e, m=m, m0=m0, n=n, r0=r0: e.matmul(
                                        ps_o[:, 1, 0:HD], pT[:, n % 2, m * P:(m + 1) * P], vg[:, m0 + m, r0:r0 + HD],
                                        start=(m0 + m == 0), stop=(m0 + m == T - 1)), ev, ov, qt, end=m == cnt - 1)
                                pv[n % 2] = mm
                            freed = ov = q.dve(lambda e, r0=r0: e.tensor_scalar(og[:, r0:r0 + HD], ps_o[:, 1, 0:HD], st[:, 3:4], None, ALU.mult),
                                               mm, rd)
                        done = q.load(att_d[bass.ds(it * P, P), c0:c0 + P], og[:], s2, ov)
                        q.put("sync", [done], lambda e: e.nop())
                        with nc.Block() as block:
                            q.emit(block)
                        nc.all_engine_barrier(sems_to_clear=loop_sems)

        def transformer_layer(L, table, next_table):
            dense = nc.values_load(flag_u[0:1, 0:1], min_val=0, max_val=1)
            with nc.If(dense):
                dense_attention(table)
            wm = load_main_weights(L) if L > 0 else (s_w, s_w.value)
            qw = load_qkv_weights(2) if L == 1 else None
            gw = load_gat() if L == 0 else None
            with ExitStack() as ph:
                ring = sbuf("gathered_edges", [P, RING, ROW], F32, ph)
                prod = sbuf("query_times_key", [P, 2, D], F32, ph)
                score = sbuf("edge_scores", [P, 2, 2 * HEADS], F32, ph)
                selT = sbuf("edge_to_node", [P, 4, P], F32, ph)
                qs = sbuf("query_parts", [P, 2, 3, D], BF16, ph)
                rden = sbuf("reciprocal_denominators", [P, 2, HEADS], F32, ph)
                att_in = prod
                n_duos = T * DUOS
                fetched, expanded, weighed, summed = {}, {}, {}, {}
                scaled = {}

                def gather(u):
                    for k in (2 * u, 2 * u + 1):
                        r = k % RING
                        fetched[k] = Q.put("pool", [last.get(("ring", r // 2))], lambda e, k=k, r=r: e.indirect_dma_start(
                            ring[:, r, 0:2 * D], None, kv_d[table], bass.IndirectOffsetOnAxis(ap=src_row[:, k:k + 1], axis=0)),
                            s_ring[r], 16)

                def split_query(t):
                    b = t % 2
                    part = lambda j: qs[:, b, j, :]
                    q, rest = q_all[:, t, :], q_rest[:]
                    free = last.get(("qs", b))
                    a = Q.act(lambda e: e.activation(part(0), q, ACT.Copy), free)
                    p = Q.pool(lambda e: e.tensor_tensor(rest, q, part(0), ALU.subtract), a, last.get("q_rest"))
                    a = Q.act(lambda e: e.activation(part(1), rest, ACT.Copy), p)
                    scaled[t] = Q.pool(lambda e: e.tensor_tensor(part(2), rest, part(1), ALU.subtract), a)
                    last["q_rest"] = scaled[t]
                    last[("q", t)] = p

                def expand(u):
                    t, bank = u // DUOS, u % 2
                    for i in range(2):
                        k = 2 * u + i - t * EDGE_TILES
                        for j in range(3):
                            m = Q.pe(lambda e, i=i, j=j, k=k: e.matmul(ps_q[:, bank, i * D:(i + 1) * D], sel[:, t, k * P:(k + 1) * P],
                                                                       qs[:, t % 2, j, :], start=(j == 0), stop=(j == 2)),
                                     scaled[t], last.get(("ps_q", bank)), end=(i == 1 and j == 2))
                    expanded[u] = m
                    last[("qs", t % 2)] = m

                def weigh(u):
                    bank, r = u % 2, 2 * u % RING
                    d = Q.dve(lambda e: e.tensor_tensor(prod[:], ring[:, r:r + 2, 0:D], ps_q[:, bank, :].rearrange("p (i c) -> p i c", i=2),
                                                        ALU.mult), expanded[u], fetched[2 * u], fetched[2 * u + 1], last.get("prod"))
                    last[("ps_q", bank)] = d
                    d = Q.dve(lambda e: e.tensor_reduce(score[:, u % 2, :], prod[:].rearrange("p i (h c) -> p (i h) c", c=HD), AX_X, ALU.add),
                              d, last.get(("score", u % 2)))
                    last["prod"] = d
                    weighed[u] = Q.act(lambda e: e.activation(ring[:, r:r + 2, 2 * D:ROW], score[:, u % 2, :].rearrange("p (i h) -> p i h", i=2),
                                                              ACT.Exp, scale=SCALE), d, fetched[2 * u], fetched[2 * u + 1])
                    last[("score", u % 2)] = weighed[u]

                def spread(u):
                    r = 2 * u % RING
                    v = ring[:, r:r + 2, D:2 * D].rearrange("p i (h c) -> p i h c", c=HD)
                    w = ring[:, r:r + 2, 2 * D:ROW].unsqueeze(3).to_broadcast([P, 2, HEADS, HD])
                    d = Q.dve(lambda e: e.tensor_tensor(v, v, w, ALU.mult), weighed[u], fetched[2 * u], fetched[2 * u + 1])
                    for i in range(2):
                        k, b = 2 * u + i, (2 * u + i) % 4
                        d = Q.dve(lambda e, k=k, b=b: e.tensor_scalar(selT[:, b, :], iota_n[:], dst_no[:, k:k + 1], None, ALU.is_equal),
                                  last.get(("selT", u % 2)))
                    summed[u] = d

                def gather_up(u):
                    t = u // DUOS
                    r = 2 * u % RING
                    for i in range(2):
                        k = 2 * u + i
                        first, final = k % EDGE_TILES == 0, k % EDGE_TILES == EDGE_TILES - 1
                        m = Q.pe(lambda e, i=i, k=k, first=first, final=final: e.matmul(
                            ps_a[:, 0:D + HEADS], selT[:, k % 4, :], ring[:, r + i, D:ROW], start=first, stop=final),
                            summed[u], last.get("ps_a"), end=i == 1)
                    last[("ring", r // 2)] = last[("selT", u % 2)] = m
                    if u % DUOS == DUOS - 1:
                        normal_out(t, m)

                def normal_out(t, m):
                    g, i = divmod(t, 2)
                    b = g % 2
                    d = Q.dve(lambda e: e.reciprocal(rden[:, i, :], ps_a[:, D:D + HEADS]), m)
                    d = Q.dve(lambda e: e.tensor_tensor(att[:, b, i, :].rearrange("p (h c) -> p h c", c=HD),
                                                        ps_a[:, 0:D].rearrange("p (h c) -> p h c", c=HD),
                                                        rden[:, i, :].unsqueeze(2).to_broadcast([P, HEADS, HD]), ALU.mult),
                              d, last.get(("att", b)))
                    last["ps_a"] = d
                    if i == 0:
                        return
                    def fetch_dense(e):
                        with e.If(dense):
                            e.dma_start(att_in[:], att_d[2 * g * P:(2 * g + 2) * P, :].rearrange("(i p) d -> p i d", p=P)).then_inc(s_dense.sem, 16)
                        with e.Else():
                            e.sem_inc(s_dense.sem, 16)

                    def take_dense(e):
                        with e.If(dense):
                            e.tensor_copy(att[:, b], att_in[:])
                        return e.memset(flag[0:1, 0:1], 0.0)

                    s_dense.value += 16
                    Q.put("sync", [last["prod"]], fetch_dense)
                    att_ready[g] = Q.dve(take_dense, (s_dense, s_dense.value), d)
                    last["prod"] = att_ready[g]

                att_ready = {}
                plan = {}
                for g in range(PAIRS):
                    if L == 0:
                        then = lambda x2, g=g: gat_input_stages(g, x2, gw)
                    elif L == 1:
                        then = lambda x2, g=g: qkv_stages(g, next_table, x2, qw)
                    else:
                        then = lambda x2, g=g: store_stage(g, x2)
                    stages = mlp_stages(g, lambda g=g: att_ready[g], wm, then)
                    for j, f in enumerate(stages):
                        plan.setdefault((g + 1) * 2 * DUOS + 3 + j * 2 * DUOS // len(stages), []).append(f)
                for u in range(AHEAD):
                    gather(u)
                split_query(0)
                split_query(1)
                expand(0)
                for u in range(max(plan) + 1):
                    if u + AHEAD < n_duos:
                        gather(u + AHEAD)
                    if u % DUOS == 0 and 2 <= u // DUOS + 1 < T:
                        split_query(u // DUOS + 1)
                    if u + 1 < n_duos:
                        expand(u + 1)
                    if u < n_duos:
                        weigh(u)
                    if 1 <= u < n_duos + 1:
                        spread(u - 1)
                    if 2 <= u < n_duos + 2:
                        gather_up(u - 2)
                    for f in plan.get(u, []):
                        f()
                if L == 1:
                    dense_test()
                finish(Q, nc, [s_w, s_w2, s_out, s_dense] + s_kv + s_ring)
            last.clear()

        g_wt = sbuf("gat_wt", [P, KD, GH])
        g_wp = sbuf("gat_wp", [GH, D])
        g_rows = sbuf("gat_rows", [P, 2 * GH + 1 + 3 * D])
        g_work = sbuf("gat_work", [P, 2, 3 * GH])
        o_bp = 2 * GH + 1

        def load_gat():
            Q.load(g_wt[:], gat_d["wt"].rearrange("(k p) n -> p k n", p=P), s_w)
            Q.load(g_wp[:], gat_d["wp"], s_w)
            return Q.load(g_rows[:], gat_d["rows"], s_w)

        def gat_layer(next_table):
            qw = load_qkv_weights(1)
            with ExitStack() as ph:
                atb = sbuf("adj_transposed_in", [P, 3, NP], F8, ph)
                ga = sbuf("gat_sums", [P, 2, GW], F32, ph)
                ones = sbuf("ones", [P, P], BF16, ph)
                ef = sbuf("gat_row_weights", [P, 6, T], F32, ph)
                htot = sbuf("h_total", [P, 3 * GH], F32, ph)
                hsum = sbuf("h_total_sum", [P, GH], F32, ph)
                nb = sbuf("neighbour_mean", [P, 2, GH], F32, ph)
                dn = sbuf("gat_denominator", [P, 2, 2], F32, ph)
                nbT = sbuf("neighbour_transposed", [GH, 2 * P], F32, ph)
                xbp = sbuf("x_plus_bp", [P, 2, D], F32, ph)
                on = Q.pool(lambda e: e.memset(ones[:], 1.0))
                for t in range(T):
                    n = min(P, n_real - t * P)
                    m = Q.pe(lambda e, t=t, n=n: e.matmul(ps_a[:, 0:3 * GH], ones[0:n, :], gh[0:n, t, 0:3 * GH],
                                                          start=(t == 0), stop=(t == T - 1)), on, end=t == T - 1)
                a = Q.act(lambda e: e.activation(htot[:], ps_a[:, 0:3 * GH], ACT.Copy), m)
                d = Q.dve(lambda e: e.tensor_tensor(hsum[:], htot[:, 0:GH], htot[:, GH:2 * GH], ALU.add), a)
                hs = Q.dve(lambda e: e.tensor_tensor(hsum[:], hsum[:], htot[:, 2 * GH:3 * GH], ALU.add), d)
                s_, mx, ee, ff, dif, fn = (ef[:, j, :] for j in range(6))
                d = Q.dve(lambda e: e.tensor_scalar(mx, gs[:], g_rows[:, 2 * GH:2 * GH + 1], None, ALU.add))
                d = Q.dve(lambda e: e.scalar_tensor_tensor(out=s_, in0=mx, scalar=0.2, in1=mx, op0=ALU.mult, op1=ALU.max), d)
                d = Q.dve(lambda e: e.tensor_scalar(mx, s_, NEG, None, ALU.max), d)
                d1 = Q.dve(lambda e: e.tensor_tensor(ee, s_, mx, ALU.subtract), d)
                d2 = Q.dve(lambda e: e.tensor_scalar(ff, mx, -1.0, NEG, ALU.mult, ALU.add), d)
                a1 = Q.act(lambda e: e.activation(ef[:, 2:4, :], ef[:, 2:4, :], ACT.Exp), d2)
                d = Q.dve(lambda e: e.tensor_tensor(dif, ee, ff, ALU.subtract), a1)
                rw = Q.dve(lambda e: e.tensor_scalar(fn, ff, float(n_real), None, ALU.mult), d)

                def aggregate(t):
                    b = t % 3
                    al = Q.load(atb[:, b, :], adjT_d[t], s_at[b], last.get(("atb", b)))
                    for m0 in range(T):
                        m = Q.pe(lambda e, m0=m0: e.matmul(ps_q[:, t % 2, 0:GW], atb[:, b, m0 * P:(m0 + 1) * P], gh[:, m0, :],
                                                           start=(m0 == 0), stop=(m0 == T - 1)), al, last.get(("ps_q", t % 2)),
                                 end=m0 == T - 1)
                    last[("atb", b)] = m
                    return m

                def rest(g, sums):
                    xp = x[:, 2 * g:2 * g + 2, :]
                    row = lambda j: g_rows[:, o_bp + j * D:o_bp + (j + 1) * D].unsqueeze(1).to_broadcast([P, 2, D])
                    s = {}

                    def mean_of(i):
                        t = 2 * g + i
                        G = lambda j: ga[:, i, j * GH:(j + 1) * GH]
                        a = Q.act(lambda e: e.activation(ga[:, i, :], ps_q[:, i, 0:GW], ACT.Copy), sums[i], last.get(("ga", i)))
                        last[("ps_q", i)] = a
                        d = Q.dve(lambda e: e.tensor_tensor(G(0), G(0), G(1), ALU.add), a)
                        d = Q.dve(lambda e: e.tensor_tensor(G(0), G(0), G(2), ALU.add), d)
                        d = Q.dve(lambda e: e.tensor_scalar(G(0), G(0), dif[:, t:t + 1], None, ALU.mult), d, rw)
                        d = Q.dve(lambda e: e.scalar_tensor_tensor(out=G(1), in0=hsum[:], scalar=ff[:, t:t + 1], in1=G(0),
                                                                   op0=ALU.mult, op1=ALU.add), d, hs)
                        c = Q.dve(lambda e: e.tensor_scalar(dn[:, i, 0:1], ga[:, i, 3 * GH:GW], dif[:, t:t + 1], fn[:, t:t + 1],
                                                            ALU.mult, ALU.add), a, rw)
                        c = Q.dve(lambda e: e.reciprocal(dn[:, i, 1:2], dn[:, i, 0:1]), c)
                        d = Q.dve(lambda e: e.tensor_scalar(nb[:, i, :], G(1), dn[:, i, 1:2], None, ALU.mult), c, d, last.get(("nb", i)))
                        last[("ga", i)] = d
                        s["nb"] = d

                    def mean():
                        for i in range(2):
                            mean_of(i)

                    def project():
                        for i in range(2):
                            m = Q.pe(lambda e, i=i: e.transpose(ps_t[0:GH, i * P:(i + 1) * P], nb[:, i, :], identf[:]), s["nb"],
                                     last.get("ps_t"), end=i == 1)
                        last[("nb", 0)] = last[("nb", 1)] = m
                        a = Q.act(lambda e: e.activation(nbT[:], ps_t[0:GH, 0:2 * P], ACT.Copy), m, last.get("nbT"))
                        last["ps_t"] = a
                        p = Q.pool(lambda e: e.tensor_tensor(xbp[:], xp, row(0), ALU.add), last.get("xbp"))
                        for i in range(2):
                            m = Q.pe(lambda e, i=i: e.matmul(ps_o[:, 0, i * D:(i + 1) * D], nbT[:, i * P:(i + 1) * P], g_wp[:],
                                                             start=True, stop=True), a, last.get("ps_o0"), end=i == 1)
                        last["nbT"] = m
                        d = Q.dve(lambda e: e.tensor_tensor(xp, ps_o[:, 0, :].rearrange("p (i n) -> p i n", i=2), xbp[:], ALU.add), m, p)
                        last["ps_o0"] = last["xbp"] = d
                        n = normalise(xp, d)
                        p = Q.pool(lambda e: e.tensor_tensor(xp, xn[:], row(1), ALU.mult), n)
                        last["xn"] = p
                        s["y"] = Q.pool(lambda e: e.tensor_tensor(xp, xp, row(2), ALU.add), p)

                    return [mean, project] + qkv_stages(g, next_table, lambda: s["y"], qw)

                for g in range(PAIRS):
                    sums = [aggregate(2 * g), aggregate(2 * g + 1)]
                    for f in rest(g, sums):
                        f()
                dense_test()
                finish(Q, nc, [s_w2] + s_at + s_kv)
            last.clear()

        transformer_layer(0, 0, None)
        gat_layer(1)
        transformer_layer(1, 1, 0)
        transformer_layer(2, 0, None)


def finish(Q, nc, dma_counters):
    for c in dma_counters:
        if c.value:
            Q.put("sync", [(c, c.value)], lambda e: e.nop())
    with nc.Block() as block:
        Q.emit(block)


def kernel(**inputs):
    import concourse.bacc as bacc
    from concourse.bass_utils import run_bass_kernel_spmd as run

    nc = bacc.Bacc("TRN2", target_bir_lowering=False, num_devices=1)
    arrays = {}

    def put(name, a):
        a = np.ascontiguousarray(a)
        arrays[name] = a
        return nc.dram_tensor(name, a.shape, mybir.dt.from_np(a.dtype), kind="ExternalInput").ap()

    x, adj = np.asarray(inputs["x"]), np.asarray(inputs["adj"])
    n, d = x.shape
    padded = -(-n // P) * P
    xp = np.zeros((padded, d), x.dtype)
    xp[:n] = x
    ap = np.eye(padded, dtype=adj.dtype)
    ap[:n, :n] = adj
    x_d, adj_d = put("x_in", xp), put("adj_in", ap)

    def columns(v):
        return np.asarray(v).reshape(-1, P).T

    def rows(v):
        return np.broadcast_to(np.asarray(v).reshape(1, -1), (P, np.asarray(v).size))

    layers = []
    for L in ("L0", "L2", "L3"):
        a = {k: np.asarray(inputs[f"{L}_gnn_{k}"]) for k in
             ("w_qkv", "w_proj", "b_proj", "w1", "b1", "w2", "b2", "g1", "be1", "g2", "be2")}
        cols = np.concatenate([columns(a[k]) for k in ("b1", "g2", "be2", "g1", "be1")], axis=1)
        rws = np.stack([rows(a["b_proj"]), rows(a["b2"])], axis=1)
        layers.append({**{k: put(f"{L}_{k}", a[k]) for k in ("w_qkv", "w_proj", "w1", "w2")},
                       "cols": put(f"{L}_cols", cols), "rows": put(f"{L}_rows", rws)})
    g = {k: np.asarray(inputs[f"L1_gnn_{k}"]) for k in ("Wt", "bt", "Wa", "ba", "Wp", "bp", "gamma", "beta")}
    gat = {"wt": put("L1_wt", g["Wt"].T), "wp": put("L1_wp", g["Wp"].T),
           "rows": put("L1_rows", np.concatenate([rows(g[k]) for k in ("bt", "Wa", "ba", "bp", "gamma", "beta")], axis=1))}
    out_d = nc.dram_tensor("out", (n, d), F32, kind="ExternalOutput").ap()
    graph_layers(nc, x_d, adj_d, layers, gat, out_d, n)
    return run(nc, [arrays], core_ids=[0]).results[0]["out"]
```

```python
from contextlib import ExitStack

import numpy as np

import concourse.bass as bass
from concourse import mybir

ALU = mybir.AluOpType
ACT = mybir.ActivationFunctionType
F32 = mybir.dt.float32
BF16 = mybir.dt.bfloat16
F8 = mybir.dt.float8e4
I32 = mybir.dt.int32
U32 = mybir.dt.uint32
AX_X = mybir.AxisListType.X
RMAX = bass.bass_isa.ReduceOp.max

P = 128
HEADS = 8
GROUP = 4
EPS = 1e-5
NEG = -9e15
MASKED = -1e30
RSQRT_MAGIC = float(0x5F3759DF)
GELU_CUBE = 0.044715
GELU_SCALE = 0.7978845608028654
SEGMENT = 256
NEIGHBOURS = 24
EDGE_TILES = 10
RING = 16
AHEAD = 5
SCORE_LIMIT = 60.0


class Counter:

    def __init__(self, sem):
        self.sem, self.value = sem, 0

    def up(self, by):
        self.value += by
        return (self, self.value)


class Queues:

    def __init__(self, ends):
        self.ends = ends
        self.steps = {k: [] for k in ("sync", "pe", "dve", "act", "pool")}

    def put(self, engine, waits, make, counter=None, by=1):
        mark = counter.up(by) if counter is not None else None
        self.steps[engine].append(([w for w in waits if w is not None], make, counter, by))
        return mark

    def pe(self, make, *waits, end=True):
        return self.put("pe", waits, make, self.ends["pe"] if end else None)

    def dve(self, make, *waits):
        return self.put("dve", waits, make, self.ends["dve"])

    def act(self, make, *waits):
        return self.put("act", waits, make, self.ends["act"])

    def pool(self, make, *waits):
        return self.put("pool", waits, make, self.ends["pool"])

    def load(self, out, in_, landed, *waits, engine="sync"):
        return self.put(engine, waits, lambda e: e.dma_start(out, in_), landed, 16)

    def emit(self, block):
        for name, on in (("sync", block.sync), ("pe", block.tensor), ("dve", block.vector),
                         ("act", block.scalar), ("pool", block.gpsimd)):
            def program(e, steps=self.steps[name]):
                passed = {}
                for waits, make, counter, by in steps:
                    for c, value in waits:
                        if passed.get(id(c), 0) < value:
                            e.wait_ge(c.sem, value)
                            passed[id(c)] = value
                    ins = make(e)
                    if counter is not None:
                        ins.then_inc(counter.sem, by)
            on(program)
            self.steps[name] = []


class Background:

    def __init__(self):
        self.chains = []

    def start(self, chain):
        self.chains.append(chain)
        return chain

    def advance(self, n=1):
        for _ in range(n):
            while self.chains:
                chain = self.chains.pop(0)
                if next(chain, self) is not self:
                    self.chains.append(chain)
                    break

    def complete(self, chain):
        while chain in self.chains:
            self.advance()


def graph_layers(nc, x_d, adj_d, layers_d, gat_d, out_d, n_real):
    NP, D = x_d.shape
    T = NP // P
    PAIRS = T // 2
    HD = D // HEADS
    KD = D // P
    FF = layers_d[0]["w1"].shape[1]
    KF = FF // P
    GH = gat_d["wt"].shape[1]
    SCALE = float(HD) ** -0.5
    GW = 3 * GH + 1

    kv_d = [nc.dram_tensor(f"kv_rows_{i}", [NP, 2 * D], F32).ap() for i in range(2)]
    adjT_d = nc.dram_tensor("adj_transposed", [T, P, NP], F8).ap()
    EDGES = EDGE_TILES * P
    SEGS = NP // SEGMENT
    DUOS = EDGE_TILES // 2
    ROW = 2 * D + HEADS
    att_d = nc.dram_tensor("dense_attention_out", [NP, D], F32).ap()

    with ExitStack() as top:
        def sem(n):
            return top.enter_context(nc.semaphore(n))

        times = {}

        def sbuf(n, shape, dt=F32, where=top):
            times[n] = times.get(n, 0) + 1
            n += f"_{times[n]}" if times[n] > 1 else ""
            return where.enter_context(nc.sbuf_tensor(n, shape, dt))

        x = sbuf("x_nodes", [P, T, D])
        q_all = sbuf("queries", [P, T, D])
        sel = sbuf("node_to_edge", [P, T, EDGES], F8)
        src_row = sbuf("edge_source_row", [P, T * EDGE_TILES], I32)
        dst_no = sbuf("edge_target_number", [P, T * EDGE_TILES])
        over = sbuf("edge_list_overflow", [P, 2, T])
        norms = sbuf("squared_norms", [P, T, 2 * HEADS])
        iota_n = sbuf("node_numbers", [P, P])
        flag = sbuf("dense_needed", [P, 2 * HEADS + 4])
        flag_u = sbuf("dense_needed_int", [P, 1], U32)
        identf = sbuf("identity_f32", [P, P])
        identb = sbuf("identity_bf16", [P, P], BF16)
        w_qkv = sbuf("w_qkv", [P, KD, 3 * D])
        w_proj = sbuf("w_proj", [P, KD, D])
        w_ff = sbuf("w_1_and_w_2", [P, KD * FF + KF * D])
        w_1 = w_ff[:, 0:KD * FF].rearrange("p (k n) -> p k n", k=KD)
        w_2 = w_ff[:, KD * FF:].rearrange("p (k n) -> p k n", k=KF)
        cols = sbuf("bias_and_norm_columns", [P, KF + 4 * KD])
        rows = sbuf("bias_rows", [P, 2, D])
        att = sbuf("attention_pair", [P, 2, D])
        xn = sbuf("normalised", [P, 2, D])
        h2T = sbuf("ff_input_transposed", [P, KD, 2 * P])
        attT = h2T
        h1T = sbuf("qkv_input_transposed", [P, KD, 2 * P])
        ffh = sbuf("ff_hidden", [P, KF, 2 * P])
        ffu = sbuf("ff_gelu_argument", [P, KF, 2 * P])
        xb = sbuf("x_plus_bias", [P, 2, 2, D])
        kv_st = sbuf("kv_to_store", [P, 2, 2 * D])
        sq = sbuf("qk_squares", [P, 2 * D])
        q_rest = sbuf("query_rest", [P, D])
        stat_2 = sbuf("norm_statistics", [P, 2, 2, 6])
        mv_2 = sbuf("mean_and_variance", [P, 2, 2, 2])
        nw_2 = sbuf("rsqrt_work", [P, 2, 6, 2])
        gh = sbuf("h_parts_and_one", [P, T, GW], BF16)
        gs = sbuf("gat_row_scores", [P, T])

        psum = lambda n, shape: top.enter_context(nc.psum_tensor(n, shape, F32))
        ps_q = psum("ps_q", [P, 2, 512])
        ps_a = psum("ps_a", [P, 512])
        ps_t = psum("ps_t", [P, 512])
        ps_w = psum("ps_w", [P, 2, 512])
        ps_o = psum("ps_o", [P, 2, 512])

        ends = {k: Counter(sem("steps_done_" + k)) for k in ("pe", "dve", "act", "pool")}
        loop_ends = {k: sem("dense_steps_done_" + k) for k in ("pe", "dve", "act", "pool")}
        loop_dma = [sem(f"dense_loaded_{i}") for i in range(3)]
        loop_sems = range(loop_ends["pe"].num, loop_dma[-1].num + 1)
        s_w = Counter(sem("weights_landed"))
        s_w2 = Counter(sem("qkv_weights_landed"))
        s_gw = Counter(sem("gat_weights_landed"))
        s_x = [Counter(sem(f"x_landed_{i}")) for i in range(2)]
        s_adj = [Counter(sem(f"adj_landed_{i}")) for i in range(2)]
        s_at = [Counter(sem(f"adj_transposed_moved_{i}")) for i in range(3)]
        s_kv = [Counter(sem(f"kv_stored_{i}")) for i in range(2)]
        s_dense = Counter(sem("dense_attention_landed"))
        s_ring = [Counter(sem(f"edges_landed_{i}")) for i in range(RING)]
        s_out = Counter(sem("out_stored"))
        Q = Queues(ends)
        bg = Background()
        last = {}

        cb1, cg2, cbe2, cg1, cbe1 = 0, KF, KF + KD, KF + 2 * KD, KF + 3 * KD

        def load_main_weights(L):
            d = layers_d[L]
            Q.load(w_proj[:], d["w_proj"].rearrange("(k p) n -> p k n", p=P), s_w)
            Q.load(cols[:, 0:cg1], d["cols"][:, 0:cg1], s_w)
            Q.load(rows[:], d["rows"], s_w)
            Q.load(w_1, d["w1"].rearrange("(k p) n -> p k n", p=P), s_w)
            return Q.load(w_2, d["w2"].rearrange("(k p) n -> p k n", p=P), s_w)

        def load_qkv_weights(L):
            d = layers_d[L]
            Q.load(cols[:, cg1:], d["cols"][:, cg1:], s_w2)
            return Q.load(w_qkv[:], d["w_qkv"].rearrange("(k p) n -> p k n", p=P), s_w2)

        def normalise(src, ready, s, of=0, out=xn, out_name="xn"):
            stat, mv, nw = stat_2[:, of], mv_2[:, of], nw_2[:, of]
            for i in range(2):
                m = Q.dve(lambda e, i=i: e.bn_stats(stat[:, i, :], src[:, i, :]), ready)
                yield
            for i in range(2):
                m = Q.dve(lambda e, i=i: e.bn_aggr(mv[:, i, :], stat[:, i, :]), m)
            yield
            var = mv[:, :, 1]
            v, hv, y, a, sh = (nw[:, j, :] for j in range(5))
            Q.dve(lambda e: e.tensor_scalar(v, var, EPS, None, ALU.add), m)
            m = Q.dve(lambda e: e.tensor_scalar(hv, var, EPS, -0.5, ALU.add, ALU.mult), m)
            yield
            m = Q.dve(lambda e: e.tensor_scalar(sh.bitcast(I32), v.bitcast(I32), 1, None, ALU.logical_shift_right), m)
            yield
            m = Q.dve(lambda e: e.tensor_scalar(y.bitcast(I32), sh.bitcast(I32), -1.0, RSQRT_MAGIC, ALU.mult, ALU.add), m)
            yield
            for _ in range(3):
                m = Q.dve(lambda e: e.tensor_tensor(a, y, y, ALU.mult), m)
                yield
                m = Q.dve(lambda e: e.tensor_tensor(a, a, hv, ALU.mult), m)
                yield
                m = Q.dve(lambda e: e.scalar_tensor_tensor(out=y, in0=a, scalar=1.5, in1=y, op0=ALU.add, op1=ALU.mult), m)
                yield
            for i in range(2):
                s["n"] = Q.dve(lambda e, i=i: e.tensor_scalar(out[:, i, :], src[:, i, :], mv[:, i, 0:1], y[:, i:i + 1],
                                                              ALU.subtract, ALU.mult), m, last.get(out_name))
            yield

        def transpose_pair(src, ready, width=D):
            for k in range(KD):
                for i in range(2):
                    o = (2 * k + i) * P
                    m = Q.pe(lambda e, k=k, i=i, o=o: e.transpose(ps_t[:, o:o + P], src[:, i, k * P:(k + 1) * P], identf[:]),
                             ready, last.get("ps_t"), end=(k, i) == (KD - 1, 1))
            return m

        def scaled_out(dst, name, g_col, b_col, turned, ready):
            for k in range(KD):
                m = Q.act(lambda e, k=k: e.activation(dst[:, k, :], ps_t[:, k * 2 * P:(k + 1) * 2 * P], ACT.Identity,
                                                      bias=cols[:, b_col + k:b_col + k + 1],
                                                      scale=cols[:, g_col + k:g_col + k + 1]),
                          turned, last.get(name), ready)
            last["ps_t"] = m
            return m

        def qkv_stages(g, table, after, qkv_w):
            s = {}

            def norm():
                s["chain"] = bg.start(normalise(x[:, 2 * g:2 * g + 2, :], after(), s, of=1))

            def turn():
                bg.complete(s["chain"])
                t = transpose_pair(xn, s["n"])
                last["xn"] = t
                s["h"] = scaled_out(h1T, "h1T", cg1, cbe1, t, qkv_w)

            def product(i, c0, c1):
                for k in range(KD):
                    m = Q.pe(lambda e, k=k: e.matmul(ps_o[:, c0 // 512, 0:c1 - c0], h1T[:, k, i * P:(i + 1) * P], w_qkv[:, k, c0:c1],
                                                     start=(k == 0), stop=(k == KD - 1)),
                             s["h"], qkv_w, last.get(f"ps_o{c0 // 512}"), end=k == KD - 1)
                last["h1T"] = m
                return m

            def query_key(i):
                t = 2 * g + i
                m = product(i, 0, 2 * D)
                Q.act(lambda e: e.activation(q_all[:, t, :], ps_o[:, 0, 0:D], ACT.Copy), m, last.get(("q", t)))
                s["sq"] = Q.act(lambda e: e.activation(sq[:], ps_o[:, 0, :], ACT.Square), m, last.get("sq"))
                s["k"] = Q.act(lambda e: e.activation(kv_st[:, i, 0:D], ps_o[:, 0, D:2 * D], ACT.Copy), m, last.get(("kv_st", i)))
                last["ps_o0"] = s["k"]

            def value(i):
                t = 2 * g + i
                m = product(i, 2 * D, 3 * D)
                last["ps_o1"] = a = Q.act(lambda e: e.activation(kv_st[:, i, D:2 * D], ps_o[:, 1, 0:D], ACT.Copy), m, last.get(("kv_st", i)))
                last["sq"] = last["norms"] = Q.dve(lambda e: e.tensor_reduce(norms[:, t, :], sq[:].rearrange("p (h c) -> p h c", c=HD),
                                                                             AX_X, ALU.add), s["sq"])
                last[("kv_st", i)] = Q.load(kv_d[table][t * P:(t + 1) * P, :], kv_st[:, i, :], s_kv[i], s["k"], a)

            return [(0, norm), (2, turn), (3, lambda: query_key(0)), (4, lambda: value(0)), (5, lambda: query_key(1)),
                    (6, lambda: value(1))]

        def gat_input_stages(g, after, gw):
            s = {}

            def turn():
                t = transpose_pair(x[:, 2 * g:2 * g + 2, :], after())
                s["h"] = Q.act(lambda e: e.activation(h1T[:].rearrange("p k n -> p (k n)"), ps_t[:], ACT.Copy), t, last.get("h1T"))
                last["ps_t"] = s["h"]

            def tile(i):
                t = 2 * g + i
                for k in range(KD):
                    m = Q.pe(lambda e, k=k: e.matmul(ps_o[:, 0, 0:GH], h1T[:, k, i * P:(i + 1) * P], g_wt[:, k, :],
                                                     start=(k == 0), stop=(k == KD - 1)), s["h"], gw, last.get("ps_o0"),
                             end=k == KD - 1)
                last["h1T"] = m
                hf = g_work[:, i, 0:GH]
                hr = g_work[:, i, GH:2 * GH]
                hw = g_work[:, i, 2 * GH:3 * GH]
                d = Q.dve(lambda e: e.tensor_tensor(hf, ps_o[:, 0, 0:GH], g_rows[:, 0:GH], ALU.add), m, gw, last.get(("gw", i)))
                last["ps_o0"] = d
                a = Q.dve(lambda e: e.tensor_tensor_reduce(hw, hf, g_rows[:, GH:2 * GH], 1.0, 0.0, ALU.mult, ALU.add,
                                                           gs[:, t:t + 1]), d)
                p = Q.pool(lambda e: e.tensor_copy(gh[:, t, 0:GH], hf), d)
                p = Q.pool(lambda e: e.tensor_tensor(hr, hf, gh[:, t, 0:GH], ALU.subtract), p, d)
                p = Q.pool(lambda e: e.tensor_copy(gh[:, t, GH:2 * GH], hr), p)
                p = Q.pool(lambda e: e.tensor_tensor(gh[:, t, 2 * GH:3 * GH], hr, gh[:, t, GH:2 * GH], ALU.subtract), p)
                last[("gw", i)] = p
                last["gs"] = a
                last["gh"] = p

            return [(2, turn), (3, lambda: tile(0)), (5, lambda: tile(1))]

        def mlp_stages(g, att_ready, wts, then, first_down, lag):
            s = {}
            b = g % 2
            xp = x[:, 2 * g:2 * g + 2, :]
            row = lambda j: rows[:, j, :].unsqueeze(1).to_broadcast([P, 2, D])

            def turn_att():
                t = transpose_pair(att[:], att_ready())
                last["att"] = t
                s["aT"] = last["ps_t"] = Q.act(lambda e: e.activation(attT[:].rearrange("p k n -> p (k n)"), ps_t[:], ACT.Copy),
                                               t, last.get("h2T"))

            def project():
                s["xb"] = Q.pool(lambda e: e.tensor_tensor(xb[:, b], xp, row(0), ALU.add), wts, last.get(("xb", b)))
                for i in range(2):
                    for k in range(KD):
                        m = Q.pe(lambda e, i=i, k=k: e.matmul(ps_w[:, 0, i * D:(i + 1) * D], attT[:, k, i * P:(i + 1) * P],
                                                              w_proj[:, k, :], start=(k == 0), stop=(k == KD - 1)),
                                 s["aT"], wts, last.get(("ps_w", 0)), end=(i == 1 and k == KD - 1))
                last["h2T"] = s["pr"] = m

            def norm():
                d = Q.dve(lambda e: e.tensor_tensor(xp, ps_w[:, 0, :].rearrange("p (i n) -> p i n", i=2), xb[:, b], ALU.add),
                          s["pr"], s["xb"])
                last[("ps_w", 0)] = d
                s["xb2"] = Q.pool(lambda e: e.tensor_tensor(xb[:, b], xp, row(1), ALU.add), d)
                s["chain"] = bg.start(normalise(xp, d, s))

            def turn():
                bg.complete(s["chain"])
                t = transpose_pair(xn, s["n"])
                last["xn"] = t
                s["h"] = scaled_out(h2T, "h2T", cg2, cbe2, t, wts)

            def up(c):
                bank = c % 2
                for j in range(2):
                    f = 2 * c + j
                    for k in range(KD):
                        m = Q.pe(lambda e, j=j, f=f, k=k: e.matmul(ps_w[:, bank, j * 2 * P:(j + 1) * 2 * P],
                                                                   w_1[:, k, f * P:(f + 1) * P], h2T[:, k, :],
                                                                   start=(k == 0), stop=(k == KD - 1)),
                                 s["h"], wts, last.get(("ps_w", bank)), end=(j == 1 and k == KD - 1))
                last["h2T"] = m
                for j in range(2):
                    f = 2 * c + j
                    src = ps_w[:, bank, j * 2 * P:(j + 1) * 2 * P]
                    Q.act(lambda e, f=f, src=src: e.activation(ffh[:, f, :], src, ACT.Identity, bias=cols[:, cb1 + f:cb1 + f + 1]),
                          m, last.get(("ffh", f // 4)))
                    a = Q.act(lambda e, f=f, src=src: e.activation(ffu[:, f, :], src, ACT.Square, bias=cols[:, cb1 + f:cb1 + f + 1]),
                              m, last.get(("ffu", f // 4)))
                last[("ps_w", bank)] = s[("up", c)] = a

            def gelu_inner(half):
                uu = ffu[:, 4 * half:4 * half + 4, :]
                d = Q.dve(lambda e: e.scalar_tensor_tensor(out=uu, in0=uu, scalar=1.0 / GELU_CUBE, in1=ffh[:, 4 * half:4 * half + 4, :],
                                                           op0=ALU.add, op1=ALU.mult), s[("up", 2 * half + 1)])
                s[("tanh", half)] = Q.act(lambda e: e.activation(uu, uu, ACT.Tanh, scale=GELU_SCALE * GELU_CUBE), d)

            def gelu_outer(half):
                hh = ffh[:, 4 * half:4 * half + 4, :]
                s[("g", half)] = Q.dve(lambda e: e.scalar_tensor_tensor(out=hh, in0=ffu[:, 4 * half:4 * half + 4, :], scalar=1.0, in1=hh,
                                                                        op0=ALU.add, op1=ALU.mult), s[("tanh", half)])
                last[("ffu", half)] = s[("g", half)]

            def down(i, half):
                for f in range(4 * half, 4 * half + 4):
                    m = Q.pe(lambda e, f=f: e.matmul(ps_o[:, 1, i * D:(i + 1) * D], ffh[:, f, i * P:(i + 1) * P],
                                                     w_2[:, f, :], start=(f == 0), stop=(f == KF - 1)),
                             s[("g", half)], wts, last.get("ps_o1"), end=f == 4 * half + 3)
                last[("ffh", half)] = s["dn"] = m

            def residual():
                s["x2"] = Q.dve(lambda e: e.scalar_tensor_tensor(out=xp, in0=ps_o[:, 1, :].rearrange("p (i n) -> p i n", i=2),
                                                                 scalar=0.5, in1=xb[:, b], op0=ALU.mult, op1=ALU.add), s["dn"], s["xb2"])
                last["ps_o1"] = last[("xb", b)] = s["x2"]

            return [(0, turn_att), (1, project), (2, norm), (5, turn), (6, lambda: up(0)), (7, lambda: up(1)),
                    (8, lambda: gelu_inner(0)), (8, lambda: up(2)), (9, lambda: gelu_outer(0)), (9, lambda: up(3)),
                    (10, lambda: gelu_inner(1)), (11, lambda: gelu_outer(1)), (first_down, lambda: down(0, 0)), (lag - 3, lambda: down(0, 1)),
                    (lag - 2, lambda: down(1, 0)), (lag - 1, lambda: down(1, 1)), (lag, residual)
                    ] + [(lag + o, f) for o, f in then(lambda: s["x2"])]

        def store_stage(g, after):
            def store():
                for i in range(2):
                    t = 2 * g + i
                    n = min(P, n_real - t * P)
                    last["out"] = Q.load(out_d[t * P:t * P + n, :], x[0:n, t, :], s_out, after())
            return [(0, store)]

        def dense_test(list_overflow=False):
            H2 = 2 * HEADS
            m = last["norms"]
            if list_overflow:
                m = Q.dve(lambda e: e.tensor_reduce(flag[:, H2 + 3:H2 + 4], over[:].rearrange("p a t -> p (a t)"), AX_X, ALU.max), last["over"])
                m = Q.pool(lambda e: e.partition_all_reduce(flag[:, H2 + 2:H2 + 3], flag[:, H2 + 3:H2 + 4], P, RMAX), m)
            m = Q.dve(lambda e: e.tensor_reduce(sq[:, 0:H2], norms[:].rearrange("p t c -> p c t"), AX_X, ALU.max), last["norms"], m)
            m = Q.pool(lambda e: e.partition_all_reduce(flag[:, 0:H2], sq[:, 0:H2], P, RMAX), m)
            m = Q.dve(lambda e: e.tensor_tensor(flag[:, 0:HEADS], flag[:, 0:HEADS], flag[:, HEADS:H2], ALU.mult), m)
            m = Q.dve(lambda e: e.tensor_reduce(flag[:, H2:H2 + 1], flag[:, 0:HEADS], AX_X, ALU.max), m)
            m = Q.dve(lambda e: e.tensor_scalar(flag[:, H2 + 1:H2 + 2], flag[:, H2:H2 + 1], (SCORE_LIMIT / SCALE) ** 2, None, ALU.is_gt), m)
            Q.dve(lambda e: e.tensor_tensor(flag_u[:], flag[:, H2 + 1:H2 + 2], flag[:, H2 + 2:H2 + 3], ALU.max), m)

        with ExitStack() as ph:
            adj_i = sbuf("adj_rows", [P, 2, NP], I32, ph)
            adj_b_2 = [sbuf("adj_rows_bf16", [P, NP], BF16, ph)[:], gh[:].rearrange("p t c -> p (t c)")[:, 0:NP]]
            at_st_2 = [sbuf("adj_transposed_tile", [P, NP], F8, ph)[:], xb[:].rearrange("p a i d -> p (a i d)").bitcast(F8)[:, 0:NP]]
            found = [w_ff[:, c:c + NP // 2].bitcast(BF16) for c in (0, KD * FF)]
            iota_e = ffh[:].rearrange("p f n -> p (f n)")[:, 0:EDGES]
            away_2 = [ffu[:].rearrange("p f n -> p (f n)")[:, 0:EDGES], sbuf("distance_from_middle", [P, EDGES], F32, ph)[:]]
            iota_s = sbuf("column_in_segment", [P, SEGMENT], BF16, ph)
            seg_base = sbuf("segment_base", [P, SEGS, 8], F32, ph)
            iota_j = sbuf("neighbour_numbers", [P, NEIGHBOURS], F32, ph)
            slot = sbuf("slot_numbers", [P, EDGE_TILES], F32, ph)
            earlier = sbuf("earlier_nodes", [P, P], BF16, ph)
            one = sbuf("one_column", [P, 1], BF16, ph)
            cand = sbuf("edge_candidates", [P, 3, SEGS * 8], F32, ph)
            nbr_2 = sbuf("neighbour_list", [P, 2, NEIGHBOURS + 2], F32, ph)
            parts_2 = sbuf("neighbour_list_parts", [P, 2, 2, NEIGHBOURS + 2], BF16, ph)
            is_edge = sbuf("is_edge", [P, NEIGHBOURS], F32, ph)
            found_n = sbuf("edges_found", [P, T], F32, ph)
            true_n = sbuf("edges_there", [P, T], F32, ph)
            end_n = sbuf("list_ends", [P, T], F32, ph)
            span = sbuf("half_length_and_middle", [P, T, 2], F32, ph)
            cnt_b = sbuf("edge_counts_bf16", [P, 1], BF16, ph)
            pick = sbuf("picked_neighbour", [P, EDGE_TILES, NEIGHBOURS], F32, ph)
            offs = sbuf("edge_offsets", [P, 3, EDGE_TILES], F32, ph)
            NB = NEIGHBOURS
            W = NB + 2
            marks = {}

            def iota(dst, pattern, base, per_partition=0):
                return Q.pool(lambda e: e.iota(dst, pattern, base=base, channel_multiplier=per_partition,
                                               allow_small_or_imprecise_dtypes=True))

            p1 = Q.pool(lambda e: e.memset(identf[:], 0.0))
            p1 = Q.pool(lambda e: e.affine_select(out=identf[:], in_=identf[:], compare_op=ALU.not_equal, fill=1.0, base=0,
                                                  pattern=[[-1, P]], channel_multiplier=1), p1)
            Q.pool(lambda e: e.tensor_copy(identb[:], identf[:]), p1)
            p1 = Q.pool(lambda e: e.memset(earlier[:], 1.0))
            Q.pool(lambda e: e.affine_select(out=earlier[:], in_=earlier[:], compare_op=ALU.is_gt, fill=0.0, base=0,
                                             pattern=[[1, P]], channel_multiplier=-1), p1)
            Q.pool(lambda e: e.memset(one[:], 1.0))
            iota(iota_s[:], [[1, SEGMENT]], 1)
            iota(seg_base[:], [[SEGMENT, SEGS], [0, 8]], 0)
            iota(iota_j[:], [[1, NB]], 0)
            iota(slot[:], [[P, EDGE_TILES]], 0, 1)
            p1 = iota(iota_e, [[1, EDGES]], 0)
            Q.pool(lambda e: e.tensor_scalar(iota_e, iota_e, 0.5, None, ALU.add), p1)
            iota(iota_n[:], [[1, P]], 1)
            iota(nbr_2[:, 0, NB + 1:NB + 2], [[0, 1]], 1, 1)
            consts = iota(nbr_2[:, 1, NB + 1:NB + 2], [[0, 1]], 1, 1)

            def load_nodes(pairs, landed, *waits):
                for g in pairs:
                    xl = Q.load(x[:, 2 * g:2 * g + 2, :], x_d[2 * g * P:(2 * g + 2) * P, :].rearrange("(i p) d -> p i d", p=P),
                                landed, *waits, engine="act")
                x_landed.update((g, xl) for g in pairs)

            x_landed = {}

            def load_adjacency(t):
                marks[("landed", t)] = Q.load(adj_i[:, t % 2, :], adj_d[t * P:(t + 1) * P, :], s_adj[t % 2], last.get(("adj_i", t % 2)))

            def adjacency_rows(t):
                b = t % 2
                last[("adj_i", b)] = marks[("rows", t)] = Q.act(lambda e: e.activation(adj_b_2[b], adj_i[:, b, :], ACT.Sign), marks[("landed", t)],
                                                                last.get(("adj_b_pe", b)), last.get(("adj_b_pool", b)))
                if t + 2 < T:
                    load_adjacency(t + 2)

            def number_columns(t):
                b = t % 2
                marks[("found", t)] = last[("adj_b_pool", b)] = Q.pool(lambda e: e.tensor_tensor(
                    found[b].rearrange("p (s c) -> p s c", c=SEGMENT), adj_b_2[b].rearrange("p (s c) -> p s c", c=SEGMENT),
                    iota_s[:].unsqueeze(1).to_broadcast([P, SEGS, SEGMENT]), ALU.mult), marks[("rows", t)], consts, last.get(("found", b)))

            def transpose_adjacency(t):
                b = t % 2
                for n, m0 in enumerate(range(0, T, 8)):
                    bank = n % 2
                    view = ps_w[:, bank, :].bitcast(BF16)
                    cnt = min(8, T - m0)
                    for m in range(cnt):
                        tr = Q.pe(lambda e, m=m, m0=m0, view=view: e.transpose(
                            view[:, m * P:(m + 1) * P], adj_b_2[b][:, (m0 + m) * P:(m0 + m + 1) * P], identb[:]),
                            marks[("rows", t)], consts, last.get(("ps_w", bank)), end=m == cnt - 1)
                    dst = at_st_2[b][:, m0 * P:(m0 + cnt) * P]
                    last[("ps_w", bank)] = Q.act(lambda e, dst=dst, view=view, cnt=cnt: e.activation(
                        dst, view[:, 0:cnt * P], ACT.Copy, saturate=False), tr, last.get(("at_st", b)), last.get(("at_st_pe", b)))
                last[("adj_b_pe", b)] = tr
                last[("at_st", b)] = Q.load(adjT_d[t], at_st_2[b], s_at[b], last[("ps_w", 0)], last[("ps_w", 1)])
                marks[("at", t)] = (last[("ps_w", 0)], last[("ps_w", 1)])

            def count_rows(t):
                for m in range(T):
                    c = Q.pe(lambda e, m=m: e.matmul(ps_q[:, 1, 0:1], at_st_2[t % 2][:, m * P:(m + 1) * P], one[:], start=(m == 0), stop=(m == T - 1)),
                             *marks[("at", t)], last.get("ps_q1"), end=m == T - 1)
                last[("at_st_pe", t % 2)] = marks[("counted", t)] = c

            def keep_counts(t):
                last["ps_q1"] = last["true_n"] = Q.act(lambda e: e.activation(true_n[:, t:t + 1], ps_q[:, 1, 0:1], ACT.Copy),
                                                       marks[("counted", t)])

            def neighbours(t):
                nbr = nbr_2[:, t % 2, :]
                fb = found[t % 2]
                for k in range(SEGS):
                    d = Q.dve(lambda e, k=k: e.max(cand[:, 0, 8 * k:8 * k + 8], fb[:, k * SEGMENT:(k + 1) * SEGMENT]), marks[("found", t)])
                    bg.advance()
                last[("found", t % 2)] = d
                flat = seg_base[:].rearrange("p s c -> p (s c)")
                d = Q.dve(lambda e: e.scalar_tensor_tensor(out=cand[:, 1, :], in0=cand[:, 0, :], scalar=0.0, in1=flat,
                                                           op0=ALU.is_gt, op1=ALU.mult), d)
                bg.advance()
                d = Q.dve(lambda e: e.tensor_tensor(cand[:, 0, :], cand[:, 0, :], cand[:, 1, :], ALU.add), d)
                bg.advance()
                for r in range(NB // 8):
                    a, b = (0, 1) if r % 2 == 0 else (1, 0)
                    d = Q.dve(lambda e, a=a, r=r: e.max(nbr[:, 8 * r:8 * r + 8], cand[:, a, :]), d, last.get(("nbr", t % 2)))
                    bg.advance()
                    if r < NB // 8 - 1:
                        d = Q.dve(lambda e, a=a, b=b, r=r: e.match_replace(out=cand[:, b, :], in_to_replace=nbr[:, 8 * r:8 * r + 8],
                                                                           in_values=cand[:, a, :], imm_value=0.0), d)
                        bg.advance()
                d = Q.dve(lambda e: e.tensor_scalar(is_edge[:], nbr[:, 0:NB], 0.0, None, ALU.is_gt), d)
                bg.advance()
                cnt = Q.dve(lambda e: e.tensor_reduce(found_n[:, t:t + 1], is_edge[:], AX_X, ALU.add), d)
                bg.advance()
                cb = Q.dve(lambda e: e.tensor_copy(cnt_b[:], found_n[:, t:t + 1]), cnt, last.get("cnt_b"))
                marks[("start", t)] = last["cnt_b"] = Q.pe(lambda e: e.matmul(ps_a[:, 0:1], earlier[:], cnt_b[:], start=True, stop=True),
                                                           cb, last.get("ps_a"))

            def place(t):
                nbr, parts = nbr_2[:, t % 2, :], parts_2[:, t % 2]
                st = Q.dve(lambda e: e.tensor_copy(nbr[:, NB:NB + 1], ps_a[:, 0:1]), marks[("start", t)])
                last["ps_a"] = st
                en = last["end_n"] = Q.dve(lambda e: e.tensor_tensor(end_n[:, t:t + 1], nbr[:, NB:NB + 1], found_n[:, t:t + 1], ALU.add), st)
                h = Q.dve(lambda e: e.tensor_scalar(span[:, t, 0:1], found_n[:, t:t + 1], 0.5, None, ALU.mult), en)
                yield
                c = Q.dve(lambda e: e.scalar_tensor_tensor(out=span[:, t, 1:2], in0=nbr[:, NB:NB + 1], scalar=-1.0, in1=span[:, t, 0:1],
                                                           op0=ALU.mult, op1=ALU.subtract), h)
                away_ready = Q.act(lambda e: e.activation(away_2[t % 2], iota_e, ACT.Abs, bias=span[:, t, 1:2]), c, consts,
                                   last.get(("away", t % 2)))
                yield
                d = Q.dve(lambda e: e.tensor_copy(parts[:, 0, :], nbr), en, last.get(("parts", t % 2)))
                yield
                pr = Q.dve(lambda e: e.tensor_tensor(parts[:, 1, :], nbr, parts[:, 0, :], ALU.subtract), d)
                last[("nbr", t % 2)] = pr
                marks[("away", t)], marks[("parts", t)] = away_ready, pr
                yield

            def one_hot(t):
                last[("away", t % 2)] = marks[("sel", t)] = Q.dve(lambda e: e.tensor_scalar(
                    sel[:, t, :], away_2[t % 2], span[:, t, 0:1], None, ALU.is_lt, saturate=False), marks[("away", t)])

            def list_edges(t):
                parts = parts_2[:, t % 2]
                for k in range(EDGE_TILES):
                    for j in range(2):
                        m = Q.pe(lambda e, k=k, j=j: e.matmul(ps_q[:, 0, k * W:(k + 1) * W], sel[:, t, k * P:(k + 1) * P], parts[:, j, :],
                                                              start=(j == 0), stop=(j == 1)), marks[("sel", t)], marks[("parts", t)], last.get("ps_q0"),
                                 end=(k == EDGE_TILES - 1 and j == 1))
                last[("parts", t % 2)] = marks[("listed", t)] = m

            def source_rows(t):
                m = marks[("listed", t)]
                G = ps_q[:, 0, 0:EDGE_TILES * W].rearrange("p (k c) -> p k c", c=W)
                d = Q.dve(lambda e: e.tensor_tensor(offs[:, 0, :], slot[:], G[:, :, NB], ALU.subtract), m)
                yield
                d = Q.dve(lambda e: e.tensor_tensor(pick[:], iota_j[:].unsqueeze(1).to_broadcast([P, EDGE_TILES, NB]),
                                                    offs[:, 0, :].unsqueeze(2).to_broadcast([P, EDGE_TILES, NB]), ALU.is_equal), d)
                yield
                d = Q.dve(lambda e: e.tensor_tensor(pick[:], pick[:], G[:, :, 0:NB], ALU.mult), d)
                yield
                d2 = Q.dve(lambda e: e.tensor_copy(dst_no[:, t * EDGE_TILES:(t + 1) * EDGE_TILES], G[:, :, NB + 1]), m)
                last["ps_q0"] = d2
                d = Q.dve(lambda e: e.tensor_reduce(offs[:, 1, :], pick[:], AX_X, ALU.add), d)
                yield
                Q.dve(lambda e: e.tensor_scalar(src_row[:, t * EDGE_TILES:(t + 1) * EDGE_TILES], offs[:, 1, :], -1.0, 0.0,
                                                ALU.add, ALU.max), d)
                yield

            load_adjacency(0)
            load_nodes(range(2), s_x[0])
            load_adjacency(1)
            qw = load_qkv_weights(0)
            norm_of, plan = {}, {}
            for g in range(PAIRS):
                norm, *others = (f for _, f in qkv_stages(g, 0, lambda g=g: x_landed[g], qw))
                norm_of[2 * g + 1] = norm
                for o, f in zip((2, 2, 3, 3, 4), others):
                    plan.setdefault(2 * g + o, []).append(f)
            adjacency_rows(0)
            number_columns(0)
            for t in range(T + 4):
                if t + 1 < T:
                    adjacency_rows(t + 1)
                if t == 1:
                    load_nodes(range(2, PAIRS), s_x[1], marks[("rows", 2)])
                if 1 <= t <= T:
                    keep_counts(t - 1)
                if t < T:
                    transpose_adjacency(t)
                chains = []
                if 2 <= t < T + 2:
                    chains.append(bg.start(place(t - 2)))
                if t >= 4:
                    chains.append(bg.start(source_rows(t - 4)))
                if t in norm_of:
                    norm_of[t]()
                if 1 <= t < T + 1:
                    neighbours(t - 1)
                if t + 1 < T:
                    number_columns(t + 1)
                for c in chains:
                    bg.complete(c)
                if 3 <= t < T + 3:
                    one_hot(t - 3)
                    list_edges(t - 3)
                for f in plan.get(t, []):
                    f()
                if t < T:
                    count_rows(t)
            Q.pool(lambda e: e.memset(gh[:], 1.0), last[("adj_b_pe", 1)], last[("adj_b_pool", 1)])
            d = Q.dve(lambda e: e.tensor_tensor(over[:, 0, :], true_n[:], found_n[:], ALU.not_equal), last["true_n"], last["end_n"])
            last["over"] = Q.dve(lambda e: e.tensor_scalar(over[:, 1, :], end_n[:], float(EDGES), None, ALU.is_gt), d)
            dense_test(list_overflow=True)
            finish(Q, nc, [s_w, s_w2] + s_x + s_adj + s_at + s_kv)
        last.clear()

        def dense_attention(table):
            S0, S1, S2 = (lambda: Counter(loop_dma[0])), (lambda: Counter(loop_dma[1])), (lambda: Counter(loop_dma[2]))
            with ExitStack() as ph:
                mask = sbuf("dense_mask", [P, NP], I32, ph)
                kT = w_ff[:, 0:NP]
                vg = sbuf("dense_values", [P, T, P], F32, ph)
                st = sbuf("dense_row_statistics", [P, 4], F32, ph)
                qp = sbuf("dense_q_tile", [P, P], F32, ph)
                qT = sbuf("dense_q_transposed", [P, P], F32, ph)
                og = sbuf("dense_out_tile", [P, P], F32, ph)
                pT = ffu[:].rearrange("p f n -> p (f n)")[:, 0:1024].rearrange("p (b n) -> p b n", b=2)
                banks = [ps_q[:, 0, :], ps_q[:, 1, :], ps_a[:], ps_t[:], ps_w[:, 0, :], ps_w[:, 1, :], ps_o[:, 0, :]]
                sc = mask[:].bitcast(F32)
                for grp in range(HEADS // GROUP):
                    c0 = grp * P
                    q = Queues({k: Counter(s) for k, s in loop_ends.items()})
                    s0, s1, s2 = S0(), S1(), S2()
                    kl = q.load(sc.rearrange("p (t c) -> p t c", c=P),
                                kv_d[table][:, c0:c0 + P].rearrange("(t p) c -> p t c", p=P), s0)
                    vl = q.load(vg[:], kv_d[table][:, D + c0:D + c0 + P].rearrange("(t p) c -> p t c", p=P), s1)
                    evac = None
                    for m0 in range(0, T, 4):
                        cnt = min(4, T - m0)
                        for m in range(cnt):
                            tr = q.pe(lambda e, m=m, m0=m0: e.transpose(ps_t[:, m * P:(m + 1) * P], sc[:, (m0 + m) * P:(m0 + m + 1) * P],
                                                                        identf[:]), kl, evac, end=m == cnt - 1)
                        evac = q.dve(lambda e, m0=m0, cnt=cnt: e.tensor_copy(kT[:, m0 * P:(m0 + cnt) * P], ps_t[:, 0:cnt * P]), tr)
                    with nc.Block() as block:
                        q.put("sync", [vl, evac], lambda e: e.nop())
                        q.emit(block)
                    nc.all_engine_barrier(sems_to_clear=loop_sems)
                    with nc.Fori(0, T) as it:
                        q = Queues({k: Counter(s) for k, s in loop_ends.items()})
                        s0, s1, s2 = S0(), S1(), S2()
                        ql = q.load(qp[:], q_all[:, bass.ds(it, 1), c0:c0 + P], s1)
                        m = q.pe(lambda e: e.transpose(ps_o[:, 1, 0:P], qp[:], identf[:]), ql)
                        qt = q.dve(lambda e: e.tensor_copy(qT[:], ps_o[:, 1, 0:P]), m)
                        freed = ov = None
                        for h in range(GROUP):
                            r0 = h * HD
                            for c in range(0, NP, 512):
                                w = min(512, NP - c)
                                m = q.pe(lambda e, c=c, w=w, r0=r0: e.matmul(banks[c // 512][:, 0:w], qT[r0:r0 + HD, :], kT[r0:r0 + HD, c:c + w],
                                                                             start=True, stop=True), qt, freed, end=c + w == NP)
                            ml = q.load(mask[:], adj_d[bass.ds(it * P, P), :], s0, freed)
                            d = q.dve(lambda e: e.tensor_scalar(sc, mask[:], 0, MASKED, ALU.is_equal, ALU.mult), ml)
                            for c in range(0, NP, 512):
                                w = min(512, NP - c)
                                d = q.dve(lambda e, c=c, w=w: e.tensor_tensor_reduce(
                                    sc[:, c:c + w], banks[c // 512][:, 0:w], sc[:, c:c + w], 1.0,
                                    -3e38 if c == 0 else st[:, 0:1], ALU.add, ALU.max, st[:, 0:1]), m, d)
                            d = q.dve(lambda e: e.tensor_scalar(st[:, 1:2], st[:, 0:1], -SCALE, None, ALU.mult), d, freed)
                            a = q.act(lambda e: e.activation(sc, sc, ACT.Exp, bias=st[:, 1:2], scale=SCALE, accum_out=st[:, 2:3]), d)
                            rd = q.dve(lambda e: e.reciprocal(st[:, 3:4], st[:, 2:3]), a)
                            pv = [None, None]
                            for n, m0 in enumerate(range(0, T, 4)):
                                cnt = min(4, T - m0)
                                for m in range(cnt):
                                    tr = q.pe(lambda e, m=m, m0=m0, n=n: e.transpose(banks[n][:, m * P:(m + 1) * P],
                                                                                    sc[:, (m0 + m) * P:(m0 + m + 1) * P], identf[:]),
                                              a, d, end=m == cnt - 1)
                                ev = q.act(lambda e, n=n, cnt=cnt: e.activation(pT[:, n % 2, 0:cnt * P], banks[n][:, 0:cnt * P], ACT.Copy),
                                           tr, pv[n % 2])
                                for m in range(cnt):
                                    mm = q.pe(lambda e, m=m, m0=m0, n=n, r0=r0: e.matmul(
                                        ps_o[:, 1, 0:HD], pT[:, n % 2, m * P:(m + 1) * P], vg[:, m0 + m, r0:r0 + HD],
                                        start=(m0 + m == 0), stop=(m0 + m == T - 1)), ev, ov, qt, end=m == cnt - 1)
                                pv[n % 2] = mm
                            freed = ov = q.dve(lambda e, r0=r0: e.tensor_scalar(og[:, r0:r0 + HD], ps_o[:, 1, 0:HD], st[:, 3:4], None, ALU.mult),
                                               mm, rd)
                        done = q.load(att_d[bass.ds(it * P, P), c0:c0 + P], og[:], s2, ov)
                        q.put("sync", [done], lambda e: e.nop())
                        with nc.Block() as block:
                            q.emit(block)
                        nc.all_engine_barrier(sems_to_clear=loop_sems)

        def transformer_layer(L, table, next_table):
            dense = nc.values_load(flag_u[0:1, 0:1], min_val=0, max_val=1)
            with nc.If(dense):
                dense_attention(table)
            with ExitStack() as ph:
                ring = sbuf("gathered_edges", [P, RING, ROW], F32, ph)
                prod = sbuf("query_times_key", [P, 2, D], F32, ph)
                score = sbuf("edge_scores", [P, 2, 2 * HEADS], F32, ph)
                selT = sbuf("edge_to_node", [P, 4, P], F32, ph)
                qs = sbuf("query_parts", [P, 2, 3, D], BF16, ph)
                rden = sbuf("reciprocal_denominators", [P, 2, HEADS], F32, ph)
                att_in = prod
                n_duos = T * DUOS
                fetched, expanded, weighed, summed = {}, {}, {}, {}
                scaled = {}

                def gather(u):
                    for k in (2 * u, 2 * u + 1):
                        r = k % RING
                        fetched[k] = Q.put("pool", [last.get(("ring", r // 2))], lambda e, k=k, r=r: e.indirect_dma_start(
                            ring[:, r, 0:2 * D], None, kv_d[table], bass.IndirectOffsetOnAxis(ap=src_row[:, k:k + 1], axis=0)),
                            s_ring[r], 16)

                def split_query(t):
                    b = t % 2
                    part = lambda j: qs[:, b, j, :]
                    q, rest = q_all[:, t, :], q_rest[:]
                    free = last.get(("qs", b))
                    a = Q.act(lambda e: e.activation(part(0), q, ACT.Copy), free)
                    p = Q.pool(lambda e: e.tensor_tensor(rest, q, part(0), ALU.subtract), a, last.get("q_rest"))
                    a = Q.act(lambda e: e.activation(part(1), rest, ACT.Copy), p)
                    scaled[t] = Q.pool(lambda e: e.tensor_tensor(part(2), rest, part(1), ALU.subtract), a)
                    last["q_rest"] = scaled[t]
                    last[("q", t)] = p

                def expand(u):
                    t, bank = u // DUOS, u % 2
                    for i in range(2):
                        k = 2 * u + i - t * EDGE_TILES
                        for j in range(3):
                            m = Q.pe(lambda e, i=i, j=j, k=k: e.matmul(ps_q[:, bank, i * D:(i + 1) * D], sel[:, t, k * P:(k + 1) * P],
                                                                       qs[:, t % 2, j, :], start=(j == 0), stop=(j == 2)),
                                     scaled[t], last.get(("ps_q", bank)), end=(i == 1 and j == 2))
                    expanded[u] = m
                    last[("qs", t % 2)] = m

                def weigh_and_spread(u, w):
                    if u is not None:
                        bank, r = u % 2, 2 * u % RING
                        d = Q.dve(lambda e: e.tensor_tensor(prod[:], ring[:, r:r + 2, 0:D], ps_q[:, bank, :].rearrange("p (i c) -> p i c", i=2),
                                                            ALU.mult), expanded[u], fetched[2 * u], fetched[2 * u + 1], last.get("prod"))
                        last[("ps_q", bank)] = d
                        bg.advance(pace)
                    if w is not None:
                        rw = 2 * w % RING
                        v = ring[:, rw:rw + 2, D:2 * D].rearrange("p i (h c) -> p i h c", c=HD)
                        wt = ring[:, rw:rw + 2, 2 * D:ROW].unsqueeze(3).to_broadcast([P, 2, HEADS, HD])
                        Q.dve(lambda e: e.tensor_tensor(v, v, wt, ALU.mult), weighed[w], fetched[2 * w], fetched[2 * w + 1])
                        bg.advance(pace)
                    if u is not None:
                        d = Q.dve(lambda e: e.tensor_reduce(score[:, u % 2, :], prod[:].rearrange("p i (h c) -> p (i h) c", c=HD), AX_X, ALU.add),
                                  d, last.get(("score", u % 2)))
                        last["prod"] = d
                        weighed[u] = Q.act(lambda e: e.activation(ring[:, r:r + 2, 2 * D:ROW], score[:, u % 2, :].rearrange("p (i h) -> p i h", i=2),
                                                                  ACT.Exp, scale=SCALE), d, fetched[2 * u], fetched[2 * u + 1])
                        last[("score", u % 2)] = weighed[u]
                        bg.advance(pace)
                    if w is not None:
                        summed[w] = Q.dve(lambda e: e.tensor_tensor(
                            selT[:, 2 * w % 4:2 * w % 4 + 2, :], iota_n[:].unsqueeze(1).to_broadcast([P, 2, P]),
                            dst_no[:, 2 * w:2 * w + 2].unsqueeze(2).to_broadcast([P, 2, P]), ALU.is_equal), last.get(("selT", w % 2)))
                        bg.advance(pace)

                def gather_up(u):
                    t = u // DUOS
                    r = 2 * u % RING
                    for i in range(2):
                        k = 2 * u + i
                        first, final = k % EDGE_TILES == 0, k % EDGE_TILES == EDGE_TILES - 1
                        m = Q.pe(lambda e, i=i, k=k, first=first, final=final: e.matmul(
                            ps_a[:, 0:D + HEADS], selT[:, k % 4, :], ring[:, r + i, D:ROW], start=first, stop=final),
                            summed[u], last.get("ps_a"), end=i == 1)
                    last[("ring", r // 2)] = last[("selT", u % 2)] = m
                    if u % DUOS == DUOS - 1:
                        normal_out(t, m)

                def normal_out(t, m):
                    g, i = divmod(t, 2)
                    d = Q.dve(lambda e: e.reciprocal(rden[:, i, :], ps_a[:, D:D + HEADS]), m)
                    d = Q.dve(lambda e: e.tensor_tensor(att[:, i, :].rearrange("p (h c) -> p h c", c=HD),
                                                        ps_a[:, 0:D].rearrange("p (h c) -> p h c", c=HD),
                                                        rden[:, i, :].unsqueeze(2).to_broadcast([P, HEADS, HD]), ALU.mult),
                              d, last.get("att"))
                    last["ps_a"] = d
                    if i == 0:
                        return
                    def fetch_dense(e):
                        with e.If(dense):
                            e.dma_start(att_in[:], att_d[2 * g * P:(2 * g + 2) * P, :].rearrange("(i p) d -> p i d", p=P)).then_inc(s_dense.sem, 16)
                        with e.Else():
                            e.sem_inc(s_dense.sem, 16)

                    def take_dense(e):
                        with e.If(dense):
                            e.tensor_copy(att[:], att_in[:])
                        return e.memset(flag[0:1, 0:1], 0.0)

                    s_dense.value += 16
                    Q.put("sync", [last["prod"]], fetch_dense)
                    att_ready[g] = Q.dve(take_dense, (s_dense, s_dense.value), d)
                    last["prod"] = att_ready[g]

                gather(0)
                split_query(0)
                expand(0)
                for u in range(1, AHEAD):
                    gather(u)
                Q.put("sync", [fetched[2 * AHEAD - 1]], lambda e: e.nop())
                wm = load_main_weights(L)
                qw = load_qkv_weights(2) if L == 1 else None
                gw = load_gat() if L == 0 else None

                att_ready = {}
                plan = {}
                pace = 3 if L == 1 else 2
                first_down, lag = (12, 16) if L == 1 else (10, 15)
                for g in range(PAIRS):
                    if L == 0:
                        then = lambda x2, g=g: gat_input_stages(g, x2, gw)
                    elif L == 1:
                        then = lambda x2, g=g: qkv_stages(g, next_table, x2, qw)
                    else:
                        then = lambda x2, g=g: store_stage(g, x2)
                    for o, f in mlp_stages(g, lambda g=g: att_ready[g], wm, then, first_down, lag):
                        plan.setdefault((g + 1) * 2 * DUOS + 3 + o, []).append(f)
                for u in range(max(plan) + 1):
                    if u + AHEAD < n_duos:
                        gather(u + AHEAD)
                    if u % DUOS == 1 and u // DUOS + 1 < T:
                        split_query(u // DUOS + 1)
                    if u + 1 < n_duos:
                        expand(u + 1)
                    weigh_and_spread(u if u < n_duos else None, u - 1 if 1 <= u <= n_duos else None)
                    if 2 <= u < n_duos + 2:
                        gather_up(u - 2)
                    for f in plan.get(u, []):
                        f()
                if L == 1:
                    dense_test()
                finish(Q, nc, [s_w, s_w2, s_gw, s_out, s_dense] + s_kv + s_ring)
            last.clear()

        g_wt = sbuf("gat_wt", [P, KD, GH])
        g_wp = sbuf("gat_wp", [GH, D])
        g_rows = sbuf("gat_rows", [P, 2 * GH + 1 + 3 * D])
        g_work = sbuf("gat_work", [P, 2, 3 * GH])
        o_bp = 2 * GH + 1

        def load_gat():
            Q.load(g_wt[:], gat_d["wt"].rearrange("(k p) n -> p k n", p=P), s_gw)
            Q.load(g_wp[:], gat_d["wp"], s_gw)
            return Q.load(g_rows[:], gat_d["rows"], s_gw)

        def gat_layer(next_table):
            qw = load_qkv_weights(1)
            with ExitStack() as ph:
                atb = sbuf("adj_transposed_in", [P, 3, NP], F8, ph)
                ga = sbuf("gat_sums", [P, 2, GW], F32, ph)
                ones = sbuf("ones", [P, P], BF16, ph)
                ef = sbuf("gat_row_weights", [P, 6, T], F32, ph)
                htot = sbuf("h_total", [P, 3 * GH], F32, ph)
                hsum = sbuf("h_total_sum", [P, GH], F32, ph)
                nb = sbuf("neighbour_mean", [P, 2, GH], F32, ph)
                dn = sbuf("gat_denominator", [P, 2, 2], F32, ph)
                nbT = sbuf("neighbour_transposed", [GH, 2 * P], F32, ph)
                on = Q.pool(lambda e: e.memset(ones[:], 1.0))
                for t in range(T):
                    n = min(P, n_real - t * P)
                    m = Q.pe(lambda e, t=t, n=n: e.matmul(ps_a[:, 0:3 * GH], ones[0:n, :], gh[0:n, t, 0:3 * GH],
                                                          start=(t == 0), stop=(t == T - 1)), on, end=t == T - 1)
                a = Q.act(lambda e: e.activation(htot[:], ps_a[:, 0:3 * GH], ACT.Copy), m)
                d = Q.dve(lambda e: e.tensor_tensor(hsum[:], htot[:, 0:GH], htot[:, GH:2 * GH], ALU.add), a)
                hs = Q.dve(lambda e: e.tensor_tensor(hsum[:], hsum[:], htot[:, 2 * GH:3 * GH], ALU.add), d)
                s_, mx, ee, ff, dif, fn = (ef[:, j, :] for j in range(6))
                d = Q.dve(lambda e: e.tensor_scalar(mx, gs[:], g_rows[:, 2 * GH:2 * GH + 1], None, ALU.add))
                d = Q.dve(lambda e: e.scalar_tensor_tensor(out=s_, in0=mx, scalar=0.2, in1=mx, op0=ALU.mult, op1=ALU.max), d)
                d = Q.dve(lambda e: e.tensor_scalar(mx, s_, NEG, None, ALU.max), d)
                d1 = Q.dve(lambda e: e.tensor_tensor(ee, s_, mx, ALU.subtract), d)
                d2 = Q.dve(lambda e: e.tensor_scalar(ff, mx, -1.0, NEG, ALU.mult, ALU.add), d)
                a1 = Q.act(lambda e: e.activation(ef[:, 2:4, :], ef[:, 2:4, :], ACT.Exp), d2)
                d = Q.dve(lambda e: e.tensor_tensor(dif, ee, ff, ALU.subtract), a1)
                rw = Q.dve(lambda e: e.tensor_scalar(fn, ff, float(n_real), None, ALU.mult), d)

                sums, fetched = {}, {}

                def fetch(t):
                    fetched[t] = Q.load(atb[:, t % 3, :], adjT_d[t], s_at[t % 3], last.get(("atb", t % 3)))

                fetch(0)
                fetch(1)

                def aggregate(t, half):
                    b = t % 3
                    if half == 0 and t + 2 < T:
                        fetch(t + 2)
                    for m0 in range(half * T // 2, (half + 1) * T // 2):
                        m = Q.pe(lambda e, m0=m0: e.matmul(ps_q[:, t % 2, 0:GW], atb[:, b, m0 * P:(m0 + 1) * P], gh[:, m0, :],
                                                           start=(m0 == 0), stop=(m0 == T - 1)), fetched[t], last.get(("ps_q", t % 2)),
                                 end=m0 == T - 1)
                    if half == 1:
                        last[("atb", b)] = sums[t] = m

                def rest(g):
                    xp = x[:, 2 * g:2 * g + 2, :]
                    row = lambda j: g_rows[:, o_bp + j * D:o_bp + (j + 1) * D].unsqueeze(1).to_broadcast([P, 2, D])
                    s = {}

                    def mean_of(i):
                        t = 2 * g + i
                        a = Q.act(lambda e: e.activation(ga[:, i, :], ps_q[:, i, 0:GW], ACT.Copy), sums[t], last.get(("ga", i)))
                        last[("ps_q", i)] = a
                        s[("mean", i)] = bg.start(mean_steps(i, t, a))

                    def mean_steps(i, t, a):
                        G = lambda j: ga[:, i, j * GH:(j + 1) * GH]
                        d = Q.dve(lambda e: e.tensor_tensor(G(0), G(0), G(1), ALU.add), a)
                        yield
                        c = Q.dve(lambda e: e.tensor_scalar(dn[:, i, 0:1], ga[:, i, 3 * GH:GW], dif[:, t:t + 1], fn[:, t:t + 1],
                                                            ALU.mult, ALU.add), a, rw)
                        yield
                        d = Q.dve(lambda e: e.tensor_tensor(G(0), G(0), G(2), ALU.add), d)
                        yield
                        c = Q.dve(lambda e: e.reciprocal(dn[:, i, 1:2], dn[:, i, 0:1]), c)
                        yield
                        d = Q.dve(lambda e: e.tensor_scalar(G(0), G(0), dif[:, t:t + 1], None, ALU.mult), d, rw)
                        yield
                        d = Q.dve(lambda e: e.scalar_tensor_tensor(out=G(1), in0=hsum[:], scalar=ff[:, t:t + 1], in1=G(0),
                                                                   op0=ALU.mult, op1=ALU.add), d, hs)
                        yield
                        d = Q.dve(lambda e: e.tensor_scalar(nb[:, i, :], G(1), dn[:, i, 1:2], None, ALU.mult), c, d, last.get(("nb", i)))
                        last[("ga", i)] = d
                        s["nb"] = d
                        yield

                    def turn_mean():
                        for i in range(2):
                            bg.complete(s[("mean", i)])
                        for i in range(2):
                            m = Q.pe(lambda e, i=i: e.transpose(ps_t[0:GH, i * P:(i + 1) * P], nb[:, i, :], identf[:]), s["nb"],
                                     last.get("ps_t"), end=i == 1)
                        last[("nb", 0)] = last[("nb", 1)] = m
                        s["nT"] = last["ps_t"] = Q.act(lambda e: e.activation(nbT[:], ps_t[0:GH, 0:2 * P], ACT.Copy), m, last.get("nbT"))

                    def project():
                        s["xb"] = Q.pool(lambda e: e.tensor_tensor(xb[:, 0], xp, row(0), ALU.add), last.get("xbp"))
                        for i in range(2):
                            m = Q.pe(lambda e, i=i: e.matmul(ps_w[:, 0, i * D:(i + 1) * D], nbT[:, i * P:(i + 1) * P], g_wp[:],
                                                             start=True, stop=True), s["nT"], last.get(("ps_w", 0)), end=i == 1)
                        last["nbT"] = s["pr"] = m

                    def norm():
                        s["norm"] = bg.start(norm_steps())

                    def norm_steps():
                        d = Q.dve(lambda e: e.tensor_tensor(xp, ps_w[:, 0, :].rearrange("p (i n) -> p i n", i=2), xb[:, 0], ALU.add),
                                  s["pr"], s["xb"])
                        last[("ps_w", 0)] = last["xbp"] = d
                        yield
                        yield from normalise(xp, d, s, out=att, out_name="att")
                        p = Q.pool(lambda e: e.tensor_tensor(xp, att[:], row(1), ALU.mult), s["n"])
                        last["att"] = p
                        s["y"] = Q.pool(lambda e: e.tensor_tensor(xp, xp, row(2), ALU.add), p)

                    def output():
                        bg.complete(s["norm"])
                        return s["y"]

                    return [(-2, lambda: mean_of(0)), (0, lambda: mean_of(1)), (2, turn_mean), (3, project), (4, norm)] + [
                        (o, f) for o, f in zip((7, 10, 11, 12, 13, 14), (f for _, f in qkv_stages(g, next_table, output, qw)))]

                plan = {}
                for g in range(PAIRS):
                    for o, f in rest(g):
                        plan.setdefault(4 * (g + 1) + o, []).append(f)
                        if o in (-2, 2):
                            plan.setdefault((4 * (g + 1) + o, "late"), []).append(plan[4 * (g + 1) + o].pop())
                for u in range(4 * PAIRS + 15):
                    for f in plan.get(u, []):
                        f()
                    if u < 2 * T:
                        aggregate(u // 2, u % 2)
                    for f in plan.get((u, "late"), []):
                        f()
                    bg.advance(14)
                dense_test()
                finish(Q, nc, [s_w2] + s_at + s_kv)
            last.clear()

        transformer_layer(0, 0, None)
        gat_layer(1)
        transformer_layer(1, 1, 0)
        transformer_layer(2, 0, None)


def finish(Q, nc, dma_counters):
    for c in dma_counters:
        if c.value:
            Q.put("sync", [(c, c.value)], lambda e: e.nop())
    with nc.Block() as block:
        Q.emit(block)


def kernel(**inputs):
    import concourse.bacc as bacc
    from concourse.bass_utils import run_bass_kernel_spmd as run

    nc = bacc.Bacc("TRN2", target_bir_lowering=False, num_devices=1)
    arrays = {}

    def put(name, a):
        a = np.ascontiguousarray(a)
        arrays[name] = a
        return nc.dram_tensor(name, a.shape, mybir.dt.from_np(a.dtype), kind="ExternalInput").ap()

    x, adj = np.asarray(inputs["x"]), np.asarray(inputs["adj"])
    n, d = x.shape
    padded = -(-n // P) * P
    xp = np.zeros((padded, d), x.dtype)
    xp[:n] = x
    ap = np.eye(padded, dtype=adj.dtype)
    ap[:n, :n] = adj
    x_d, adj_d = put("x_in", xp), put("adj_in", ap)

    def columns(v):
        return np.asarray(v).reshape(-1, P).T

    def rows(v):
        return np.broadcast_to(np.asarray(v).reshape(1, -1), (P, np.asarray(v).size))

    layers = []
    for L in ("L0", "L2", "L3"):
        a = {k: np.asarray(inputs[f"{L}_gnn_{k}"]) for k in
             ("w_qkv", "w_proj", "b_proj", "w1", "b1", "w2", "b2", "g1", "be1", "g2", "be2")}
        cols = np.concatenate([columns(a[k]) for k in ("b1", "g2", "be2", "g1", "be1")], axis=1)
        rws = np.stack([rows(a["b_proj"]), rows(a["b2"])], axis=1)
        layers.append({**{k: put(f"{L}_{k}", a[k]) for k in ("w_qkv", "w_proj", "w1", "w2")},
                       "cols": put(f"{L}_cols", cols), "rows": put(f"{L}_rows", rws)})
    g = {k: np.asarray(inputs[f"L1_gnn_{k}"]) for k in ("Wt", "bt", "Wa", "ba", "Wp", "bp", "gamma", "beta")}
    gat = {"wt": put("L1_wt", g["Wt"].T), "wp": put("L1_wp", g["Wp"].T),
           "rows": put("L1_rows", np.concatenate([rows(g[k]) for k in ("bt", "Wa", "ba", "bp", "gamma", "beta")], axis=1))}
    out_d = nc.dram_tensor("out", (n, d), F32, kind="ExternalOutput").ap()
    graph_layers(nc, x_d, adj_d, layers, gat, out_d, n)
    return run(nc, [arrays], core_ids=[0]).results[0]["out"]
```
